# Optimizing a Trainium2 kernel written in Bass

```python
import numpy as np
import jax
import jax.numpy as jnp

def _softmax(x, axis=-1):
    return jax.nn.softmax(x, axis=axis)
def _gelu(x):
    return jax.nn.gelu(x, approximate=True)
def _silu(x):
    return jax.nn.silu(x)
def _sigmoid(x):
    return jax.nn.sigmoid(x)
def _layernorm(x, axis=-1, eps=1e-5):
    m = jnp.mean(x, axis=axis, keepdims=True)
    v = jnp.var(x, axis=axis, keepdims=True)
    return (x - m) / jnp.sqrt(v + eps)
def _scatter_add(tgt, idx, src, axis=0):
    return tgt.at[idx].add(src)
def _segment_sum(src, seg, n):
    return jax.ops.segment_sum(src, seg, n)

kernel_name = 'mk_conv_preact_d2_conv_nhwc256_021224'

def setup_inputs(seed: int = 0):
    np.random.seed(seed)
    _w = jnp.asarray
    def _rec_inputs():
        import jax
        import jax.numpy as jnp
        _gk = jax.random.key(seed)
        x = -0.0003957 + 1 * jax.random.normal(jax.random.fold_in(_gk, 1), (16, 56, 56, 256), jnp.float32)
        return x
    x = _rec_inputs()
    def _L0_conv_setup():
        import jax, jax.numpy as jnp
        import numpy as np

        def _threshold(w):
            return 0.7 * jnp.mean(jnp.abs(w))

        def _compute_alpha(w):
            t = _threshold(w)
            kept = jnp.where(w > t, w, 0.0) + jnp.where(w < -t, w, 0.0)
            kept_abs = jnp.abs(kept)
            n = jnp.sum((kept_abs > 0).astype(w.dtype))
            return jnp.sum(kept_abs) / n

        def _ternary(w):
            t = _threshold(w)
            return jnp.sign(jnp.sign(w + t) + jnp.sign(w - t))
        key = jax.random.key(seed)
        k1, k2 = jax.random.split(key)
        x = jax.random.normal(k1, (16, 56, 56, 256), dtype=jnp.float32)
        W = jax.random.normal(k2, (3, 3, 256, 256), dtype=jnp.float32) * 0.02
        b = jnp.zeros((256,), dtype=jnp.float32)
        return {'x': x, 'W': W, 'b': b}
    _L0_conv_all = _L0_conv_setup()
    _L0_conv_in = {k: v for k, v in _L0_conv_all.items() if k in ('W', 'b', )}
    del _L0_conv_all

    def _L1_conv_setup():
        import jax, jax.numpy as jnp
        import numpy as np
        from jax import lax
        B_, H_, W_, C_ = (32, 56, 56, 256)
        RED = 16
        STATE = 16
        EPS = 1e-05

        def _s6(m, A, d_w, d_b, B_w, B_b, C_w, C_b):
            delta = jax.nn.softplus(m @ d_w.T + d_b)
            Bm = m @ B_w.T + B_b
            Cm = m @ C_w.T + C_b
            dA = jnp.exp(delta[..., None] * A)
            dBx = (delta * m)[..., None] * Bm[:, :, None, :]
            a_t = jnp.moveaxis(dA, 1, 0)
            b_t = jnp.moveaxis(dBx, 1, 0)
            c_t = jnp.moveaxis(Cm[:, :, None, :], 1, 0)

            def step(h, abc):
                a, b, c = abc
                h = a * h + b
                y = jnp.sum(h * c, axis=-1)
                return (h, y)
            h0 = jnp.zeros_like(a_t[0])
            _, ys = lax.scan(step, h0, (a_t, b_t, c_t))
            return jnp.moveaxis(ys, 0, 1)
        key = jax.random.key(seed)
        ks = jax.random.split(key, 10)
        x = jax.random.normal(ks[0], (B_, H_, W_, C_), jnp.float32)
        ca_w1 = jax.random.normal(ks[1], (C_ // RED, C_), jnp.float32) * 0.05
        ca_w2 = jax.random.normal(ks[2], (C_, C_ // RED), jnp.float32) * 0.05
        lsa_w = jax.random.normal(ks[3], (7, 7, 2, 1), jnp.float32) * 0.05
        A = -jnp.exp(jax.random.normal(ks[4], (1, STATE), jnp.float32) * 0.5)
        d_w = jax.random.normal(ks[5], (1, 1), jnp.float32) * 0.5
        d_b = jnp.zeros((1,), jnp.float32)
        B_w = jax.random.normal(ks[6], (STATE, 1), jnp.float32) * 0.5
        B_b = jnp.zeros((STATE,), jnp.float32)
        C_w = jax.random.normal(ks[7], (STATE, 1), jnp.float32) * 0.5
        C_b = jnp.zeros((STATE,), jnp.float32)
        bn_gamma = jnp.ones((C_,), jnp.float32)
        bn_beta = jnp.zeros((C_,), jnp.float32)
        return dict(x=x, ca_w1=ca_w1, ca_w2=ca_w2, lsa_w=lsa_w, A=A, d_w=d_w, d_b=d_b, B_w=B_w, B_b=B_b, C_w=C_w, C_b=C_b, bn_gamma=bn_gamma, bn_beta=bn_beta)
    _L1_conv_all = _L1_conv_setup()
    _L1_conv_in = {k: v for k, v in _L1_conv_all.items() if k in ('ca_w1', 'ca_w2', 'lsa_w', 'A', 'd_w', 'd_b', 'B_w', 'B_b', 'C_w', 'C_b', 'bn_gamma', 'bn_beta', )}
    del _L1_conv_all

    return {
        "x": x,
        "L0_conv_W": _L0_conv_in["W"],
        "L0_conv_b": _L0_conv_in["b"],
        "L1_conv_ca_w1": _L1_conv_in["ca_w1"],
        "L1_conv_ca_w2": _L1_conv_in["ca_w2"],
        "L1_conv_lsa_w": _L1_conv_in["lsa_w"],
        "L1_conv_A": _L1_conv_in["A"],
        "L1_conv_d_w": _L1_conv_in["d_w"],
        "L1_conv_d_b": _L1_conv_in["d_b"],
        "L1_conv_B_w": _L1_conv_in["B_w"],
        "L1_conv_B_b": _L1_conv_in["B_b"],
        "L1_conv_C_w": _L1_conv_in["C_w"],
        "L1_conv_C_b": _L1_conv_in["C_b"],
        "L1_conv_bn_gamma": _L1_conv_in["bn_gamma"],
        "L1_conv_bn_beta": _L1_conv_in["bn_beta"],
    }

def reference(x, L0_conv_W, L0_conv_b, L1_conv_ca_w1, L1_conv_ca_w2, L1_conv_lsa_w, L1_conv_A, L1_conv_d_w, L1_conv_d_b, L1_conv_B_w, L1_conv_B_b, L1_conv_C_w, L1_conv_C_b, L1_conv_bn_gamma, L1_conv_bn_beta):
    import jax
    import jax.numpy as jnp
    def _L0_conv_ref(x, W, b):
        import jax, jax.numpy as jnp
        import numpy as np

        def _threshold(w):
            return 0.7 * jnp.mean(jnp.abs(w))

        def _compute_alpha(w):
            t = _threshold(w)
            kept = jnp.where(w > t, w, 0.0) + jnp.where(w < -t, w, 0.0)
            kept_abs = jnp.abs(kept)
            n = jnp.sum((kept_abs > 0).astype(w.dtype))
            return jnp.sum(kept_abs) / n

        def _ternary(w):
            t = _threshold(w)
            return jnp.sign(jnp.sign(w + t) + jnp.sign(w - t))
        alpha = _compute_alpha(W)
        w_q = alpha * _ternary(W)
        y = jax.lax.conv_general_dilated(x, w_q, window_strides=(1, 1), padding='SAME', dimension_numbers=('NHWC', 'HWIO', 'NHWC'))
        return jax.nn.relu(y + b)

    def _L1_conv_ref(x, ca_w1, ca_w2, lsa_w, A, d_w, d_b, B_w, B_b, C_w, C_b, bn_gamma, bn_beta):
        import jax, jax.numpy as jnp
        import numpy as np
        from jax import lax
        B_, H_, W_, C_ = (32, 56, 56, 256)
        RED = 16
        STATE = 16
        EPS = 1e-05

        def _s6(m, A, d_w, d_b, B_w, B_b, C_w, C_b):
            delta = jax.nn.softplus(m @ d_w.T + d_b)
            Bm = m @ B_w.T + B_b
            Cm = m @ C_w.T + C_b
            dA = jnp.exp(delta[..., None] * A)
            dBx = (delta * m)[..., None] * Bm[:, :, None, :]
            a_t = jnp.moveaxis(dA, 1, 0)
            b_t = jnp.moveaxis(dBx, 1, 0)
            c_t = jnp.moveaxis(Cm[:, :, None, :], 1, 0)

            def step(h, abc):
                a, b, c = abc
                h = a * h + b
                y = jnp.sum(h * c, axis=-1)
                return (h, y)
            h0 = jnp.zeros_like(a_t[0])
            _, ys = lax.scan(step, h0, (a_t, b_t, c_t))
            return jnp.moveaxis(ys, 0, 1)
        Bn, H, W, C = x.shape
        avg = jnp.mean(x, axis=(1, 2))
        mx = jnp.max(x, axis=(1, 2))
        fc = lambda v: jax.nn.relu(v @ ca_w1.T) @ ca_w2.T
        ca_gate = jax.nn.sigmoid(fc(avg) + fc(mx))[:, None, None, :]
        xc = x * ca_gate
        m = jnp.mean(xc, axis=-1, keepdims=True).reshape(Bn, H * W, 1)
        y = _s6(m, A, d_w, d_b, B_w, B_b, C_w, C_b).reshape(Bn, H, W, 1)
        ma = xc * jax.nn.sigmoid(y)
        feat = jnp.concatenate([jnp.mean(xc, axis=-1, keepdims=True), jnp.max(xc, axis=-1, keepdims=True)], axis=-1)
        s = lax.conv_general_dilated(feat, lsa_w, (1, 1), 'SAME', dimension_numbers=('NHWC', 'HWIO', 'NHWC'))
        sa = xc * jax.nn.sigmoid(s)
        x2 = ma + sa
        mean = jnp.mean(x2, axis=(0, 1, 2))
        var = jnp.var(x2, axis=(0, 1, 2))
        out = (x2 - mean) * lax.rsqrt(var + EPS) * bn_gamma + bn_beta
        return jax.nn.relu(out)

    def _gn(v, G=32, eps=1e-5):
        B_, H_, W_, C_ = v.shape
        g = v.reshape(B_, H_, W_, G, C_ // G)
        m = jnp.mean(g, axis=(1, 2, 4), keepdims=True)
        s = jnp.var(g, axis=(1, 2, 4), keepdims=True)
        return ((g - m) / jnp.sqrt(s + eps)).reshape(v.shape)

    def _ln_c(v, eps=1e-6):
        m = jnp.mean(v, axis=-1, keepdims=True)
        s = jnp.var(v, axis=-1, keepdims=True)
        return (v - m) / jnp.sqrt(s + eps)

    def _ln_t(v, eps=1e-5):
        m = jnp.mean(v, axis=-1, keepdims=True)
        s = jnp.var(v, axis=-1, keepdims=True)
        return (v - m) / jnp.sqrt(s + eps)

    def _to_tokens(v):
        B_, H_, W_, C_ = v.shape
        return v.reshape(B_, H_ * W_, C_)
    def _from_tokens(t, like):
        return t.reshape(like.shape)

    x = x + _L0_conv_ref(_gn(x), L0_conv_W, L0_conv_b)
    x = x + _L1_conv_ref(_gn(x), L1_conv_ca_w1, L1_conv_ca_w2, L1_conv_lsa_w, L1_conv_A, L1_conv_d_w, L1_conv_d_b, L1_conv_B_w, L1_conv_B_b, L1_conv_C_w, L1_conv_C_b, L1_conv_bn_gamma, L1_conv_bn_beta)
    return x


_drawn_inputs = setup_inputs


def setup_inputs(seed=0):
    import zlib

    import numpy as np

    out = dict(_drawn_inputs(seed))
    spreads = {'L0_conv_b': (0.0, 0.1),
     'L1_conv_B_b': (0.0, 2.0),
     'L1_conv_C_b': (0.0, 2.0),
     'L1_conv_bn_gamma': (1.0, 0.2),
     'L1_conv_bn_beta': (0.0, 0.1)}
    factors = {'L1_conv_ca_w1': 4.498,
     'L1_conv_ca_w2': 4.351,
     'L1_conv_lsa_w': 3.617,
     'L1_conv_A': 64.0,
     'L1_conv_B_w': 64.0,
     'L1_conv_C_w': 64.0}
    for name, (base, spread) in spreads.items():
        noise = np.random.default_rng([zlib.crc32(name.encode()), seed]).standard_normal(out[name].shape)
        drawn = base * np.exp(spread * noise) if base else spread * noise
        out[name] = jnp.asarray(drawn.astype(out[name].dtype))
    for name, factor in factors.items():
        out[name] = (out[name] * factor).astype(out[name].dtype)
    return out
```

```python
from contextlib import ExitStack

import concourse.bass as bass
from concourse import mybir

F32 = mybir.dt.float32
F16 = mybir.dt.float16
I32 = mybir.dt.int32
ALU = mybir.AluOpType
ACT = mybir.ActivationFunctionType
AX_X = mybir.AxisListType.X

P = 128
HF = 2
H = W = 56
PX = H * W
CH = 8
R = H // CH
CW = R * W
UN = CH * HF
NT = 4
TW = CW // NT
TAPS = 9
ST = 16
RED = 16
GS = 8
K7 = 7
PAD7 = K7 // 2
BAND = 2 * H - 1
MAXROW = 64
SLOTS = 4
CLAMP = -80.0

PREP = {9: [0], 10: [1, 2], 11: [3], 12: [4], 14: [5]}
PREP_OWN = [6, 7]
WSTAT = {9: [0], 10: [1], 11: [2], 12: [3], 13: [4], 14: [5], 15: [6, 7]}
GATE0 = 7


class Live:

    def __init__(self, i, n_images):
        self.conv = 0 <= i < n_images
        self.next = 0 <= i + 1 < n_images
        self.a = 0 <= i - 1 < n_images
        self.b = 0 <= i - 2 < n_images


def iterations(eng, n_images, work):
    full = Live(2, 4)
    for i in range(-1, 2):
        work(i, Live(i, n_images))
    with eng.Fori(2, n_images - 1) as i:
        work(i, full)
    for i in range(n_images - 1, n_images + 2):
        work(i, Live(i, n_images))


def wait(eng, sem, value):
    if not isinstance(value, int) or value > 0:
        eng.wait_ge(sem, value)


def build_kernel(nc, x, w, bias, w1, w2, lsa, scal, bn, out):
    NB = x.shape[0]
    assert NB % SLOTS == 0 and NB >= 4
    NPIX = float(NB * PX)
    WCOLS = TAPS * HF * 2 * P

    ctx = ExitStack()
    with ctx:
        def sb(name, shape, dt=F32):
            return ctx.enter_context(nc.sbuf_tensor(name, shape, dt))

        def bank(name, n=1):
            return ctx.enter_context(nc.psum_tensor(name, [P, n, 512], F32))

        def sem(name):
            return ctx.enter_context(nc.semaphore(name))

        x1_dram = nc.dram_tensor("x1_dram", (NB, HF, P, PX), F32, kind="Internal").ap()
        feat_dram = nc.dram_tensor("feat_dram", (2, PX), F32, kind="Internal").ap()
        g_dram = nc.dram_tensor("g_dram", (NB, PX), F32, kind="Internal").ap()
        band_dram = nc.dram_tensor("band_dram", (P, K7, BAND), F32, kind="Internal").ap()

        xs = sb("xs", [P, SLOTS, HF, PX])
        hl = sb("hl", [P, 2, HF, H + 2, W + 2], F16)
        tern = sb("tern", [P, TAPS, HF, 2 * P], F16)
        xn = sb("xn", [P, 2, HF, CW])
        rl = sb("rl", [P, 4, CW])
        xc = sb("xc", [P, 2, HF, CW])
        xm = sb("xm", [P, 2, CW])
        xa = sb("xa", [P, 2, CW])
        wk = sb("wk", [P, 2, HF, CW])
        gB = sb("gB", [P, PX])

        ident = sb("ident", [P, P])
        ones = sb("ones", [P, P])
        gmat = sb("gmat", [P, P])
        meanm = sb("meanm", [P, CH, P])
        selr = sb("selr", [P, R, H])
        lw = sb("lw", [P, K7, K7, 2])
        band = gB[:, 0:K7 * BAND].rearrange("p (a b) -> p a b", b=BAND)
        toep = sb("toep", [P, K7, H])
        rmask = sb("rmask", [1, P])
        pidx = sb("pidx", [P, 1], I32)
        pj = sb("pj", [P, 1], I32)
        pjf = sb("pjf", [P, 1])
        tgt = sb("tgt", [P, R])
        iot = sb("iot", [P, H])

        w1T = sb("w1T", [P, HF, RED])
        w2T = sb("w2T", [RED, HF * P])
        biasc = sb("biasc", [P, HF])
        sv = sb("sv", [P, 7])
        bnp = sb("bnp", [P, 2, HF])
        wred = sb("wred", [P, TAPS * HF])
        wstat = sb("wstat", [P, 8])
        alpha = sb("alpha", [P, 1])
        tick = sb("tick", [1, 1])

        st = [sb(f"st{q}", [P, HF, CH, 6]) for q in range(2)]
        stw = sb("stw", [P, HF, CH, 6])
        mv = [sb(f"mv{q}", [P, HF, 2]) for q in range(2)]
        gm = [sb(f"gm{q}", [P, HF]) for q in range(2)]
        dv = [sb(f"dv{q}", [P, HF]) for q in range(2)]
        dq = [sb(f"dq{q}", [P, HF]) for q in range(2)]
        vv = [sb(f"vv{q}", [P, HF]) for q in range(3)]
        lnv = [sb(f"lnv{q}", [P, HF]) for q in range(3)]
        r0 = [sb(f"r0{q}", [P, HF]) for q in range(3)]
        nt = [sb(f"nt{q}", [P, HF]) for q in range(3)]
        rs = [sb(f"rs{q}", [P, HF]) for q in range(3)]
        mx1 = sb("mx1", [P, CH, HF])
        fmx = sb("fmx", [P, HF])
        fd = sb("fd", [P, HF, 2])
        fv = sb("fv", [P, HF, 2])
        hr = sb("hr", [RED, 2])
        hs = sb("hs", [RED, 1])
        garg = sb("garg", [P, HF])
        gexp = sb("gexp", [P, HF])
        gden = sb("gden", [P, HF])
        gate = sb("gate", [P, HF])
        kcur = sb("kcur", [P, HF])
        nb = sb("nb", [P, HF])
        mxT = sb("mxT", [P, NT * CH])
        mxr = sb("mxr", [NT * CH, TW])
        feat = sb("feat", [P, W + 2 * PAD7])

        ms = sb("ms", [P, CW])
        zs = sb("zs", [P, CW])
        nz = sb("nz", [P, CW])
        es = sb("es", [P, CW])
        us = sb("us", [P, CW])
        ls = sb("ls", [P, CW])
        de = sb("de", [P, CW])
        dA = sb("dA", [P, CW])
        sumd = sb("sumd", [P, 1])
        pe_ = sb("pend", [P, 1])
        rp = sb("rp", [1, P])
        rh = sb("rh", [1, P])
        rH = sb("rH", [1, P])
        hin = sb("hin", [1, P])
        hinc = sb("hinc", [P, 1])
        sy = sb("sy", [H, 2, W])
        sye = sb("sye", [H, 2, W])
        syd = sb("syd", [H, 2, W])
        syr = sb("syr", [H, 2, W])
        g56 = sb("g56", [H, W])
        mwt = sb("mwt", [P, HF, 2])

        gmA = sb("gmA", [P, NB, HF])
        kA = sb("kA", [P, NB, HF])
        mwA = sb("mwA", [P, NB, HF, 2])
        bm = sb("bm", [P, NB, HF])
        bq = sb("bq", [P, NB, HF])
        bs = sb("bs", [P, HF])
        bmean = sb("bmean", [P, HF])
        bscale = sb("bscale", [P, HF])
        bA = sb("bA", [P, NB, HF])
        bAs = sb("bAs", [P, SLOTS, HF])
        bB = sb("bB", [P, HF])

        cv = bank("cv", 4)
        Mb = bank("Mb")
        TR = bank("TR")
        SA = bank("SA")
        SB = bank("SB")
        M = Mb[:, 0, 0:CW]
        S7 = Mb[0:H, 0, 0:W]
        TRv = TR[0:TW, 0, :].rearrange("p (t c) -> p t c", t=NT)
        ROWP = SB[0:1, 0, 128:256]
        ROWH = SB[0:1, 0, 256:384]
        HIN = SB[:, 0, 384:385]
        Y56 = SB[0:H, 0, 400:400 + W]

        params = sem("params"); w_loaded = sem("w_loaded"); lw_loaded = sem("lw_loaded")
        pool_const = sem("pool_const"); dve_const = sem("dve_const")
        w_sum = sem("w_sum"); w_tot = sem("w_tot"); w_cnt = sem("w_cnt"); w_cnt_tot = sem("w_cnt_tot")
        w_ready = sem("w_ready"); band_ready = sem("band_ready"); band_stored = sem("band_stored")
        toep_ready = sem("toep_ready"); pad_ready = sem("pad_ready")
        x_loaded = sem("x_loaded"); x1_stored = sem("x1_stored")
        xn_done = sem("xn_done"); hi_done = sem("hi_done"); lo_done = sem("lo_done")
        conv_done = sem("conv_done"); relu_done = sem("relu_done"); x1_done = sem("x1_done")
        mean_in = [sem(f"mean_in{q}") for q in range(2)]
        mean_out = [sem(f"mean_out{q}") for q in range(2)]
        var_in = [sem(f"var_in{q}") for q in range(2)]
        var_out = [sem(f"var_out{q}") for q in range(2)]
        v_ready = [sem(f"v_ready{q}") for q in range(3)]
        rs_guess = [sem(f"rs_guess{q}") for q in range(3)]
        fc1_in = sem("fc1_in"); fc1_out = sem("fc1_out"); fc2_in = sem("fc2_in"); fc2_out = sem("fc2_out")
        gate_arg = sem("gate_arg"); gate_exp = sem("gate_exp"); gate_done = sem("gate_done")
        xc_done = sem("xc_done"); pair_done = sem("pair_done"); tr_done = sem("tr_done"); tr_read = sem("tr_read")
        mxt_done = sem("mxt_done"); mxr_ready = sem("mxr_ready"); m_ready = sem("m_ready")
        nz_ready = sem("nz_ready"); e_ready = sem("e_ready"); u_ready = sem("u_ready"); l_ready = sem("l_ready")
        delta_ready = sem("delta_ready"); decay_ready = sem("decay_ready"); ends_ready = sem("ends_ready")
        rows_out = sem("rows_out"); hin_ready = sem("hin_ready"); hin_out = sem("hin_out")
        hc_ready = sem("hc_ready"); y_done = sem("y_done"); c7_done = sem("c7_done"); s_taken = sem("s_taken")
        sy_ready = sem("sy_ready"); sye_ready = sem("sye_ready"); g_ready = sem("g_ready")
        feat_stored = sem("feat_stored"); feat_loaded = sem("feat_loaded")
        g_stored = sem("g_stored"); g_spread = sem("g_spread"); w_done = sem("w_done")
        bn_ready = sem("bn_ready"); grow_loaded = [sem(f"grow_loaded{k}") for k in range(2)]
        x1_back = [sem(f"x1_back{k}") for k in range(SLOTS)]
        out_stored = [sem(f"out_stored{k}") for k in range(SLOTS)]
        spread = sem("spread"); prod_done = sem("prod_done"); act_done = sem("act_done")
        add_dve = sem("add_dve"); add_pool = sem("add_pool")

        C2 = 2 * CW
        N2 = CH // 2 * HF
        RING2 = 4
        ring2 = [xn[:, :, :, :].rearrange("p a h c -> p (a h c)"), xc[:, :, :, :].rearrange("p a h c -> p (a h c)")]
        growt = gB

        def chunk(slot, h, c, n=1):
            return xs[:, slot, h, c * CW:(c + n) * CW]

        def rows(ap):
            return ap.rearrange("p (r w) -> p r w", w=W)

        def step_buf(k):
            return ring2[k // 2][:, (k % 2) * C2:(k % 2) * C2 + C2]

        block = ctx.enter_context(nc.Block())

        @block.sync
        def _(sp):
            sp.dma_start(xs[:, 2, :, :].rearrange("p h x -> p (h x)")[:, 0:WCOLS].rearrange("p (t m) -> p t m", m=2 * P),
                         w.rearrange("t p m -> p t m")).then_inc(w_loaded, 16)
            sp.dma_start(biasc[:, :], bias).then_inc(params, 16)
            sp.dma_start(w1T[:, :, :], w1).then_inc(params, 16)
            sp.dma_start(w2T[:, :], w2).then_inc(params, 16)
            sp.dma_start(sv[:, :], scal).then_inc(params, 16)
            sp.dma_start(bnp[:, :, :], bn).then_inc(params, 16)
            sp.dma_start(lw[:, :, :, :].rearrange("p a b c -> p (a b c)"), lsa.partition_broadcast(P)).then_inc(lw_loaded, 16)
            sp.wait_ge(band_ready, 1)
            sp.dma_start(band_dram, band).then_inc(band_stored, 16)
            sp.wait_ge(band_stored, 16)
            for c in range(2):
                src = bass.AP(tensor=band_dram.tensor, offset=c * MAXROW * K7 * BAND + H - 1,
                              ap=[[K7 * BAND - 1, H], [BAND, K7], [1, H]])
                sp.dma_start(toep[c * MAXROW:c * MAXROW + H, :, :], src).then_inc(toep_ready, 16)

            def work(i, live):
                if live.next:
                    n = i + 1
                    if not isinstance(i, int) or i >= 2:
                        sp.wait_ge(x1_stored, 16 * (i - 1))
                        sp.wait_ge(m_ready, i - 1)
                    elif i == 0:
                        sp.wait_ge(w_ready, 1)
                    wait(sp, x_loaded, 16 * n)
                    sp.dma_start(xs[:, n % SLOTS, :, :], x[n].rearrange("h p x -> p h x")).then_inc(x_loaded, 16)
                if live.b:
                    n = i - 2
                    sp.wait_ge(m_ready, n + 1)
                    sp.dma_start(feat_dram[0].rearrange("(j x) -> j x", j=CH), ms[0:CH, :]).then_inc(feat_stored, 16)
                    sp.wait_ge(mxr_ready, n + 1)
                    sp.dma_start(feat_dram[1].rearrange("(b x) -> b x", x=TW), mxr[:, :]).then_inc(feat_stored, 16)
                    sp.wait_ge(feat_stored, 32 * (n + 1))
                    for c in range(2):
                        sp.dma_start(feat[c * MAXROW:c * MAXROW + H, PAD7:PAD7 + W],
                                     feat_dram[c].rearrange("(a b) -> a b", b=W)).then_inc(feat_loaded, 16)
                if live.a:
                    sp.wait_ge(x1_done, UN * i)
                    wait(sp, x1_stored, 16 * (i - 1))
                    sp.dma_start(x1_dram[i - 1].rearrange("h p x -> p h x"),
                                 xs[:, (i - 1) % SLOTS, :, :]).then_inc(x1_stored, 16)
                if live.b:
                    n = i - 2
                    sp.wait_ge(g_ready, n + 1)
                    sp.dma_start(g_dram[n].rearrange("(a b) -> a b", b=W), g56[:, :]).then_inc(g_stored, 16)
                    sp.wait_ge(g_stored, 16 * (n + 1))
                    sp.dma_start(gB[:, :], g_dram[n].partition_broadcast(P)).then_inc(g_spread, 16)

            def fix(i, live):
                work(i, live)

            iterations(sp, NB, fix)

            sp.wait_ge(x1_stored, 16 * NB)
            sp.wait_ge(w_done, CH * NB)

            def grow(n, k, count):
                sp.dma_start(growt[32 * k:32 * k + 1, :], g_dram[n].rearrange("(a b) -> a b", a=1)).then_inc(grow_loaded[k], 16)

            def out_image(n, s):
                sp.dma_start(out[n].rearrange("h p x -> p h x"), xs[:, s, :, :]).then_inc(out_stored[s], 16)

            def finish(t, s, n, more):
                sp.wait_ge(add_dve, (t + 1) * (N2 // 2))
                sp.wait_ge(add_pool, (t + 1) * (N2 // 2))
                out_image(n, s)

            def refill(t, s, n4):
                sp.wait_ge(out_stored[s], 16 * (t // SLOTS + 1) if isinstance(t, int) else 16 * (t // SLOTS + 1))
                sp.dma_start(xs[:, s, :, :], x1_dram[n4].rearrange("h p x -> p h x")).then_inc(x1_back[s], 16)

            for k in range(2):
                grow(NB - SLOTS + k, k, 1)
            for q in range(1):
                for s in range(SLOTS):
                    finish(s, s, NB - SLOTS + s, True)
                    grow((NB - SLOTS + s + 2) % NB, s % 2, 0)
                    refill(s, s, s)
            def middle(q):
                for s in range(SLOTS):
                    finish(SLOTS * (q + 1) + s, s, SLOTS * q + s, True)
                    grow(SLOTS * q + s + 2, s % 2, 0)
                    sp.wait_ge(out_stored[s], 16 * (q + 2))
                    sp.dma_start(xs[:, s, :, :], x1_dram[SLOTS * q + s + SLOTS].rearrange("h p x -> p h x")).then_inc(x1_back[s], 16)

            if NB // SLOTS > 2:
                with sp.Fori(0, NB // SLOTS - 2) as q:
                    middle(q)
            for s in range(SLOTS):
                t = NB - SLOTS + s
                finish(t, s, t - SLOTS, False)
                if s < 2:
                    grow(t - SLOTS + 2, s, 0)
            for s in range(SLOTS):
                sp.wait_ge(out_stored[s], 16 * (NB // SLOTS))

        @block.gpsimd
        def _(pool):
            pool.memset(ident[:, :], 0.0).then_inc(pool_const, 1)
            pool.memset(gmat[:, :], 1.0 / GS).then_inc(pool_const, 1)
            pool.memset(ones[:, :], 1.0).then_inc(pool_const, 1)
            pool.iota(pidx[:, :], pattern=[[0, 1]], base=0, channel_multiplier=1).then_inc(pool_const, 1)
            pool.iota(iot[:, :], pattern=[[1, H]], base=0, channel_multiplier=0,
                      allow_small_or_imprecise_dtypes=True).then_inc(pool_const, 1)
            pool.wait_ge(pool_const, 5)
            pool.affine_select(out=ident[:, :], in_=ident[:, :], compare_op=ALU.not_equal, fill=1.0, base=0,
                               pattern=[[-1, P]], channel_multiplier=1).then_inc(pool_const, 1)
            g3 = gmat[:, :].rearrange("p (a b) -> p a b", b=GS)
            pool.affine_select(out=g3, in_=g3, compare_op=ALU.is_ge, fill=0.0, base=0,
                               pattern=[[-GS, P // GS], [0, GS]], channel_multiplier=1).then_inc(pool_const, 1)
            pool.wait_ge(pool_const, 7)
            pool.affine_select(out=g3, in_=g3, compare_op=ALU.is_ge, fill=0.0, base=GS - 1,
                               pattern=[[GS, P // GS], [0, GS]], channel_multiplier=-1).then_inc(pool_const, 1)

            def residual(n, u):
                b, o = divmod(u, HF)
                pool.wait_ge(relu_done, UN * n + u + 1)
                pool.wait_ge(w_ready, 1)
                at = chunk(n % SLOTS, o, b)
                pool.tensor_tensor(at, at, rl[:, u % 4, :], ALU.add).then_inc(x1_done, 1)

            def work(i, live):
                if live.a:
                    residual(i - 1, UN - 1)
                if live.conv:
                    for u in range(UN - 1):
                        residual(i, u)

            iterations(pool, NB, work)

            def add2(t, s, c2, h):
                k = N2 * t + HF * c2 + h
                pool.wait_ge(act_done, k + 1)
                at = chunk(s, h, 2 * c2, 2)
                pool.tensor_tensor(at, at, step_buf(k_static(s, c2, h)), ALU.add).then_inc(add_pool, 1)

            def k_static(s, c2, h):
                return (N2 * s + HF * c2 + h) % RING2

            def phase2(t, s):
                for c2 in range(CH // 2):
                    add2(t, s, c2, 1)

            for s in range(SLOTS):
                phase2(s, s)
            with pool.Fori(1, NB // SLOTS) as q:
                for s in range(SLOTS):
                    phase2(SLOTS * q + s, s)

        @block.scalar
        def _(act):
            def relu(n, u):
                b, o = divmod(u, HF)
                act.wait_ge(conv_done, UN * n + u + 1)
                wait(act, x1_done, UN * n + u - 3)
                act.wait_ge(w_ready, 1)
                act.activation(rl[:, u % 4, :], cv[:, u % 4, 0:CW], ACT.Relu, bias=biasc[:, o:o + 1],
                               scale=alpha[:, 0:1]).then_inc(relu_done, 1)

            def high(n, c):
                act.wait_ge(xn_done, CH * n + c + 1)
                wait(act, conv_done, UN * (n - 1) + 2 * min(c + 1, CH - 1) + 2)
                act.wait_ge(pad_ready, 1)
                act.copy(hl[:, 0, :, 1 + R * c:1 + R * (c + 1), 1:1 + W],
                         xn[:, c % 2, :, :].rearrange("p h (r w) -> p h r w", w=W)).then_inc(hi_done, 1)

            def rsqrt_guess(q, count):
                act.wait_ge(v_ready[q], count)
                act.activation(lnv[q][:, :], vv[q][:, :], ACT.Ln)
                act.drain()
                act.activation(r0[q][:, :], lnv[q][:, :], ACT.Exp, scale=-0.5).then_inc(rs_guess[q], 1)

            def gated(n, c):
                act.wait_ge(gate_done, n + 1)
                wait(act, pair_done, CH * n + c - 1)
                act.wait_ge(w_ready, 1)
                for h in range(HF):
                    last = act.activation(xc[:, c % 2, h, :], chunk(n % SLOTS, h, c), ACT.Identity,
                                          bias=nb[:, h:h + 1], scale=kcur[:, h:h + 1])
                last.then_inc(xc_done, 1)

            def work(i, live):
                for u in range(UN):
                    if u == 0 and live.conv:
                        for c in PREP_OWN:
                            if c == PREP_OWN[0] and live.a:
                                relu(i - 1, UN - 1)
                            high(i, c)
                    elif u == 0 and live.a:
                        relu(i - 1, UN - 1)
                    if u > 0 and live.conv:
                        relu(i, u - 1)
                    if live.b and u == 0:
                        act.wait_ge(nz_ready, i - 1)
                        act.activation(es[:, :], nz[:, :], ACT.Exp).then_inc(e_ready, 1)
                    if live.b and u == 1:
                        act.wait_ge(u_ready, i - 1)
                        act.activation(ls[:, :], us[:, :], ACT.Ln).then_inc(l_ready, 1)
                    if live.b and u == 2:
                        act.wait_ge(delta_ready, i - 1)
                        act.activation(dA[:, :], de[:, :], ACT.Exp, scale=sv[:, 0:1])
                        act.activation(pe_[:, :], sumd[:, :], ACT.Exp, scale=sv[:, 0:1]).then_inc(decay_ready, 1)
                    if live.a and u == 3:
                        rsqrt_guess(1, i)
                    if live.b and u == 6:
                        act.wait_ge(sy_ready, i - 1)
                        act.activation(sye[:, :, :], sy[:, :, :], ACT.Exp, scale=-1.0).then_inc(sye_ready, 1)
                    if live.a and u == 6:
                        act.wait_ge(gate_arg, i)
                        act.activation(gexp[:, :], garg[:, :], ACT.Exp, scale=-1.0).then_inc(gate_exp, 1)
                    if live.next and u == 8:
                        rsqrt_guess(0, i + 2)
                    if live.a and GATE0 <= u < GATE0 + CH:
                        gated(i - 1, u - GATE0)
                    if live.next:
                        for c in PREP.get(u, []):
                            high(i + 1, c)

            act.wait_ge(params, 5 * 16)
            iterations(act, NB, work)
            rsqrt_guess(2, 1)

            def phase2(t, s):
                for c2 in range(CH // 2):
                    for h in range(HF):
                        k = N2 * t + HF * c2 + h
                        act.wait_ge(prod_done, k + 1)
                        act.wait_ge(bn_ready, 1)
                        buf = step_buf((N2 * s + HF * c2 + h) % RING2)
                        act.activation(buf, buf, ACT.Relu, bias=bB[:, h:h + 1],
                                       scale=bAs[:, s, h:h + 1]).then_inc(act_done, 1)

            for s in range(SLOTS):
                phase2(s, s)
            with act.Fori(1, NB // SLOTS) as q:
                for s in range(SLOTS):
                    phase2(SLOTS * q + s, s)

        @block.tensor
        def _(pe):
            def conv(n, u):
                b, o = divmod(u, HF)
                wait(pe, relu_done, UN * n + u - 3)
                if o == 0:
                    pe.wait_ge(lo_done, CH * n + min(b + 1, CH - 1) + 1)
                first = True
                for k in range(HF):
                    for tap in range(TAPS):
                        dy, dx = divmod(tap, 3)
                        for part in range(2):
                            last = pe.matmul(cv[:, u % 4, 0:CW], tern[:, tap, k, o * P:(o + 1) * P],
                                             hl[:, part, k, R * b + dy:R * b + dy + R, dx:dx + W],
                                             start=first, stop=(k == 1 and tap == TAPS - 1 and part == 1))
                            first = False
                last.then_inc(conv_done, 1)

            def group_mean(q, count):
                pe.wait_ge(mean_in[q], count)
                pe.matmul(SA[:, 0, 4 * q:4 * q + 2], gmat[:, :], mv[q][:, :, 0], start=True, stop=True).then_inc(mean_out[q], 1)

            def group_var(q, count):
                pe.wait_ge(var_in[q], count)
                pe.matmul(SA[:, 0, 4 * q + 2:4 * q + 4], gmat[:, :], dv[q][:, :], start=True, stop=True).then_inc(var_out[q], 1)

            def reduce_channels(n, c):
                pe.wait_ge(pair_done, CH * n + c + 1)
                wait(pe, tr_read, CH * n + c)
                if c == 0:
                    wait(pe, s_taken, n)
                    wait(pe, m_ready, n)
                pe.matmul(M, meanm[:, c, :], xa[:, c % 2, :], start=(c == 0), stop=(c == CH - 1))
                for k in range(NT):
                    last = pe.transpose(TR[0:TW, 0, k * P:(k + 1) * P], xm[:, c % 2, k * TW:(k + 1) * TW], ident[:, :])
                last.then_inc(tr_done, 1)

            def work(i, live):
                for u in range(UN):
                    if live.conv:
                        conv(i, u)
                    if live.b:
                        n = i - 2
                        if u == 0:
                            pe.wait_ge(tr_read, CH * (n + 1))
                            pe.wait_ge(m_ready, n + 1)
                            pe.transpose(SB[0:NT * CH, 0, 0:TW], mxT[0:TW, :], ident[0:TW, 0:TW]).then_inc(mxt_done, 1)
                        if u == 3:
                            pe.wait_ge(mxr_ready, n + 1)
                            pe.wait_ge(ends_ready, n + 1)
                            pe.matmul(ROWP, pe_[:, :], ident[:, :], start=True, stop=True)
                            pe.matmul(ROWH, nz[:, CW - 1:CW], ident[:, :], start=True, stop=True).then_inc(rows_out, 1)
                        if u == 4:
                            pe.wait_ge(feat_loaded, 32 * (n + 1))
                            pe.wait_ge(m_ready, n + 1)
                            for dx in range(K7):
                                last = pe.matmul(S7, toep[0:MAXROW + H, dx, :], feat[0:MAXROW + H, dx:dx + W],
                                                 start=(dx == 0), stop=(dx == K7 - 1))
                            last.then_inc(c7_done, 1)
                            pe.wait_ge(hin_ready, n + 1)
                            pe.matmul(HIN, hin[:, :], ones[0:1, 0:1], start=True, stop=True).then_inc(hin_out, 1)
                        if u == 5:
                            pe.wait_ge(hc_ready, n + 1)
                            for r in range(R):
                                last = pe.matmul(Y56, selr[:, r, :], es[:, r * W:(r + 1) * W],
                                                 start=(r == 0), stop=(r == R - 1))
                            last.then_inc(y_done, 1)
                    if live.a:
                        n = i - 1
                        if u == 1:
                            group_mean(1, n + 1)
                        if u == 2:
                            group_var(1, n + 1)
                        if u == 4:
                            pe.wait_ge(fc1_in, n + 1)
                            for h in range(HF):
                                last = pe.matmul(SA[0:RED, 0, 8:10], w1T[:, h, :], fv[:, h, :], start=(h == 0), stop=(h == 1))
                            last.then_inc(fc1_out, 1)
                        if u == 5:
                            pe.wait_ge(fc2_in, n + 1)
                            for h in range(HF):
                                last = pe.matmul(SA[:, 0, 10 + h:11 + h], w2T[:, h * P:(h + 1) * P], hs[:, :], start=True, stop=True)
                            last.then_inc(fc2_out, 1)
                        if GATE0 <= u < GATE0 + CH:
                            reduce_channels(n, u - GATE0)
                    if live.next:
                        if u == 6:
                            if live.a:
                                pe.wait_ge(gate_arg, i)
                            group_mean(0, i + 2)
                        if u == 7:
                            group_var(0, i + 2)

            pe.wait_ge(params, 5 * 16)
            pe.wait_ge(pool_const, 8)
            pe.wait_ge(dve_const, 1)
            pe.wait_ge(toep_ready, 32)
            pe.wait_ge(w_sum, 1)
            pe.matmul(SA[:, 0, 0:1], ones[:, :], wstat[:, 0:1], start=True, stop=True).then_inc(w_tot, 1)
            pe.wait_ge(w_cnt, 1)
            pe.matmul(SA[:, 0, 2:4], ones[:, :], wstat[:, 2:4], start=True, stop=True).then_inc(w_cnt_tot, 1)
            pe.wait_ge(w_ready, 1)
            iterations(pe, NB, work)

            def phase2(t, s, count):
                k = s % 2
                pe.wait_ge(grow_loaded[k], count)
                for c2 in range(CH // 2):
                    wait(pe, prod_done, N2 * t + HF * (c2 - 1))
                    for e in range(2):
                        last = pe.matmul(cv[:, 2 * (c2 % 2) + e, 0:CW], ones[32 * k:32 * k + 1, :],
                                         growt[32 * k:32 * k + 1, (2 * c2 + e) * CW:(2 * c2 + e + 1) * CW],
                                         start=True, stop=True)
                    last.then_inc(spread, 1)

            for s in range(SLOTS):
                phase2(s, s, 16 * (s // 2 + 1))
            with pe.Fori(1, NB // SLOTS) as q:
                for s in range(SLOTS):
                    phase2(SLOTS * q + s, s, 16 * (2 * q + s // 2 + 1))

        @block.vector
        def _(v):
            wv = xs[:, 2, :, :].rearrange("p h x -> p (h x)")[:, 0:WCOLS]
            wa = xs[:, 3, :, :].rearrange("p h x -> p (h x)")[:, 0:WCOLS]
            wj = xs[:, 1, :, :].rearrange("p h x -> p (h x)")[:, 0:WCOLS]
            v.memset(hl[:, :, :, :, :], 0.0).then_inc(pad_ready, 1)
            v.memset(feat[:, :], 0.0)
            v.memset(toep[:, :, :], 0.0)
            v.memset(band, 0.0)
            v.memset(meanm[:, :, :], 0.0)
            v.memset(rmask[:, :], 1.0)
            v.memset(hin[:, :], 0.0)
            v.drain()
            v.memset(rmask[:, 0:P:CH], 0.0)
            for c in range(CH):
                v.memset(meanm[:, c, c:P:CH], 1.0 / (HF * P))
            v.wait_ge(lw_loaded, 16)
            for c in range(2):
                a = c * MAXROW
                for dy in range(K7):
                    last = v.tensor_copy(band[a:a + H, :, H - 1 + PAD7 - dy], lw[a:a + H, dy, :, c])
            last.then_inc(band_ready, 1)
            v.wait_ge(w_loaded, 16)
            v.tensor_reduce(wred[:, :], wv.rearrange("p (a b) -> p a b", b=2 * P), AX_X, ALU.add, apply_absolute_value=True)
            v.drain()
            v.tensor_reduce(wstat[:, 0:1], wred[:, :], AX_X, ALU.add).then_inc(w_sum, 1)
            v.scalar_tensor_tensor(wa, wv, -1.0, wv, ALU.mult, ALU.max)
            v.wait_ge(pool_const, 8)
            v.tensor_scalar(pj[:, :], pidx[:, :], CH - 1, None, ALU.bitwise_and)
            v.drain()
            v.tensor_copy(pjf[:, :], pj[:, :])
            v.drain()
            for r in range(R):
                v.tensor_scalar(tgt[:, r:r + 1], pjf[:, :], float(R), float(r), ALU.mult, ALU.add)
            v.drain()
            for r in range(R):
                last = v.tensor_scalar(selr[:, r, :], iot[:, :], tgt[:, r:r + 1], None, ALU.is_equal)
            last.then_inc(dve_const, 1)
            v.wait_ge(w_tot, 1)
            v.tensor_scalar(wstat[:, 1:2], SA[:, 0, 0:1], 1.0 / (WCOLS * P), 0.7, ALU.mult, ALU.mult)
            v.drain()
            v.tensor_scalar(wstat[:, 4:5], wstat[:, 1:2], -1.0, None, ALU.mult)
            v.tensor_scalar(wj, wa, wstat[:, 1:2], None, ALU.is_gt, ALU.add, accum_out=wstat[:, 3:4])
            v.drain()
            v.scalar_tensor_tensor(wj, wa, wstat[:, 1:2], wa, ALU.is_gt, ALU.mult, accum_out=wstat[:, 2:3])
            v.drain()
            v.tensor_scalar(wj, wv, wstat[:, 4:5], None, ALU.is_le).then_inc(w_cnt, 1)
            v.drain()
            v.scalar_tensor_tensor(tern[:, :, :, :].rearrange("p t k m -> p (t k m)"), wv, wstat[:, 1:2], wj,
                                   ALU.is_ge, ALU.subtract)
            v.wait_ge(w_cnt_tot, 1)
            v.tensor_copy(wstat[:, 5:7], SA[:, 0, 2:4])
            v.drain()
            v.reciprocal(wstat[:, 7:8], wstat[:, 6:7])
            v.drain()
            v.tensor_tensor(alpha[:, :], wstat[:, 5:6], wstat[:, 7:8], ALU.mult).then_inc(w_ready, 1)
            v.wait_ge(params, 5 * 16)

            def held(sem_, value):
                v.drain()
                v.wait_ge(sem_, value)
                v.memset(tick[:, :], 0.0)

            def x_stats(n, cs):
                held(x_loaded, 16 * (n + 1))
                for c in cs:
                    for h in range(HF):
                        v.bn_stats(st[0][:, h, c, :], chunk(n % SLOTS, h, c))

            def x1_stats(n, b):
                held(x1_done, UN * n + 2 * b + 2)
                for h in range(HF):
                    v.bn_stats(st[1][:, h, b, :], chunk(n % SLOTS, h, b))
                v.tensor_reduce(mx1[:, b, :], xs[:, n % SLOTS, :, b * CW:(b + 1) * CW], AX_X, ALU.max)

            def gn_aggregate(q):
                v.drain()
                for h in range(HF):
                    last = v.bn_aggr(mv[q][:, h, :], st[q][:, h, :, :].rearrange("p c s -> p (c s)"))
                last.then_inc(mean_in[q], 1)

            def gn_deviation(q, count):
                v.wait_ge(mean_out[q], count)
                v.tensor_copy(gm[q][:, :], SA[:, 0, 4 * q:4 * q + 2])
                v.drain()
                v.tensor_tensor(dq[q][:, :], mv[q][:, :, 0], gm[q][:, :], ALU.subtract)
                v.drain()
                v.tensor_tensor(dq[q][:, :], dq[q][:, :], dq[q][:, :], ALU.mult)
                v.drain()
                v.tensor_tensor(dv[q][:, :], dq[q][:, :], mv[q][:, :, 1], ALU.add).then_inc(var_in[q], 1)

            def gn_variance(q, count):
                v.wait_ge(var_out[q], count)
                v.tensor_scalar(vv[q][:, :], SA[:, 0, 4 * q + 2:4 * q + 4], 1e-5, None, ALU.add).then_inc(v_ready[q], 1)

            def newton(q, count):
                v.wait_ge(rs_guess[q], count)
                v.tensor_tensor(nt[q][:, :], r0[q][:, :], r0[q][:, :], ALU.mult)
                v.drain()
                v.tensor_tensor(nt[q][:, :], nt[q][:, :], vv[q][:, :], ALU.mult)
                v.drain()
                v.tensor_scalar(nt[q][:, :], nt[q][:, :], -0.5, 1.5, ALU.mult, ALU.add)
                v.drain()
                v.tensor_tensor(rs[q][:, :], r0[q][:, :], nt[q][:, :], ALU.mult)
                v.drain()

            def prep(n, c):
                v.wait_ge(x_loaded, 16 * (n + 1))
                for h in range(HF):
                    last = v.tensor_scalar(xn[:, c % 2, h, :], chunk(n % SLOTS, h, c), gm[0][:, h:h + 1],
                                           rs[0][:, h:h + 1], ALU.subtract, ALU.mult)
                last.then_inc(xn_done, 1)

            def low(n, c):
                v.wait_ge(hi_done, CH * n + c + 1)
                rows_ = slice(1 + R * c, 1 + R * (c + 1))
                for h in range(HF):
                    last = v.tensor_tensor(hl[:, 1, h, rows_, 1:1 + W], rows(xn[:, c % 2, h, :]),
                                           hl[:, 0, h, rows_, 1:1 + W], ALU.subtract)
                last.then_inc(lo_done, 1)

            def pair(n, c):
                v.wait_ge(xc_done, CH * n + c + 1)
                wait(v, tr_done, CH * n + c - 1)
                v.tensor_tensor(xm[:, c % 2, :], xc[:, c % 2, 0, :], xc[:, c % 2, 1, :], ALU.max)
                v.tensor_tensor(xa[:, c % 2, :], xc[:, c % 2, 0, :], xc[:, c % 2, 1, :], ALU.add).then_inc(pair_done, 1)

            def max_pixels(n, c):
                v.wait_ge(tr_done, CH * n + c + 1)
                if c == 0:
                    wait(v, mxt_done, n)
                v.tensor_reduce(mxT[0:TW, NT * c:NT * (c + 1)], TRv, AX_X, ALU.max).then_inc(tr_read, 1)

            def bn_chunk(n, c):
                if c == 0:
                    v.wait_ge(g_spread, 16 * (n + 1))
                for h in range(HF):
                    v.scalar_tensor_tensor(wk[:, c % 2, h, :], chunk(n % SLOTS, h, c), gmA[:, n, h:h + 1],
                                           gB[:, c * CW:(c + 1) * CW], ALU.subtract, ALU.mult)
                v.drain()
                for h in range(HF):
                    last = v.bn_stats(stw[:, h, c, :], wk[:, c % 2, h, :])
                last.then_inc(w_done, 1)
                if c == CH - 1:
                    v.drain()
                    for h in range(HF):
                        v.bn_aggr(mwt[:, h, :], stw[:, h, :, :].rearrange("p c s -> p (c s)"))
                    v.drain()
                    v.tensor_copy(mwA[:, n, :, :], mwt[:, :, :])

            def stage_b(n, u):
                if u == 0:
                    v.wait_ge(tr_done, CH * (n + 1))
                    v.tensor_copy(ms[:, :], M).then_inc(m_ready, 1)
                    v.drain()
                    v.tensor_scalar(zs[:, :], ms[:, :], sv[:, 5:6], sv[:, 6:7], ALU.mult, ALU.add)
                    v.drain()
                    v.scalar_tensor_tensor(nz[:, :], zs[:, :], -1.0, zs[:, :], ALU.mult, ALU.min).then_inc(nz_ready, 1)
                if u == 1:
                    v.wait_ge(mxt_done, n + 1)
                    v.tensor_copy(mxr[:, :], SB[0:NT * CH, 0, 0:TW]).then_inc(mxr_ready, 1)
                    v.wait_ge(e_ready, n + 1)
                    v.tensor_scalar(us[:, :], es[:, :], 1.0, None, ALU.add).then_inc(u_ready, 1)
                    v.drain()
                    v.scalar_tensor_tensor(de[:, :], us[:, :], 1.0, es[:, :], ALU.subtract, ALU.subtract)
                    v.drain()
                    v.scalar_tensor_tensor(zs[:, :], zs[:, :], 0.0, de[:, :], ALU.max, ALU.subtract)
                    v.drain()
                if u == 2:
                    v.wait_ge(l_ready, n + 1)
                    v.scalar_tensor_tensor(de[:, :], zs[:, :], 1.0, ls[:, :], ALU.mult, ALU.add,
                                           accum_out=sumd[:, :]).then_inc(delta_ready, 1)
                    v.tensor_scalar(us[:, :], ms[:, :], sv[:, 1:2], sv[:, 2:3], ALU.mult, ALU.add)
                    v.drain()
                    v.tensor_tensor(zs[:, :], de[:, :], ms[:, :], ALU.mult)
                    v.drain()
                    v.tensor_tensor(ls[:, :], zs[:, :], us[:, :], ALU.mult)
                    v.drain()
                if u == 3:
                    v.wait_ge(decay_ready, n + 1)
                    v.tensor_tensor_scan(nz[:, :], dA[:, :], ls[:, :], 0.0, ALU.mult, ALU.add).then_inc(ends_ready, 1)
                if u == 4:
                    v.wait_ge(rows_out, n + 1)
                    v.tensor_tensor(rp[:, :], ROWP, rmask[:, :], ALU.mult)
                    v.tensor_copy(rh[:, :], ROWH)
                    v.drain()
                    v.tensor_tensor_scan(rH[:, :], rp[:, :], rh[:, :], 0.0, ALU.mult, ALU.add)
                    v.drain()
                    v.tensor_tensor(hin[:, 1:P], rH[:, 0:P - 1], rmask[:, 1:P], ALU.mult).then_inc(hin_ready, 1)
                if u == 5:
                    v.wait_ge(c7_done, n + 1)
                    v.tensor_scalar(sy[:, 1, :], S7, CLAMP, None, ALU.max).then_inc(s_taken, 1)
                    v.tensor_scalar(us[:, :], ms[:, :], sv[:, 3:4], sv[:, 4:5], ALU.mult, ALU.add)
                    v.wait_ge(hin_out, n + 1)
                    v.tensor_copy(hinc[:, :], HIN)
                    v.drain()
                    v.tensor_tensor_scan(zs[:, :], dA[:, :], ls[:, :], hinc[:, 0:1], ALU.mult, ALU.add)
                    v.drain()
                    v.tensor_tensor(es[:, :], zs[:, :], us[:, :], ALU.mult).then_inc(hc_ready, 1)
                if u == 6:
                    v.wait_ge(y_done, n + 1)
                    v.tensor_scalar(sy[:, 0, :], Y56, CLAMP, None, ALU.max).then_inc(sy_ready, 1)
                if u == 7:
                    v.wait_ge(sye_ready, n + 1)
                    v.tensor_scalar(syd[:, :, :], sye[:, :, :], 1.0, None, ALU.add)
                    v.drain()
                    v.reciprocal(syr[:, :, :], syd[:, :, :])
                    v.drain()
                    v.tensor_tensor(g56[:, :], syr[:, 0, :], syr[:, 1, :], ALU.add).then_inc(g_ready, 1)
                for c in WSTAT.get(u, []):
                    bn_chunk(n, c)

            def stage_a(n, u):
                if u == 0:
                    x1_stats(n, CH - 1)
                if u == 1:
                    gn_aggregate(1)
                if u == 2:
                    v.tensor_reduce(fmx[:, :], mx1[:, :, :].rearrange("p c h -> p h c"), AX_X, ALU.max)
                    gn_deviation(1, n + 1)
                if u == 3:
                    gn_variance(1, n + 1)
                    v.tensor_copy(gmA[:, n, :], gm[1][:, :])
                    v.tensor_tensor(fd[:, :, 0], mv[1][:, :, 0], gm[1][:, :], ALU.subtract)
                    v.tensor_tensor(fd[:, :, 1], fmx[:, :], gm[1][:, :], ALU.subtract)
                    v.drain()
                if u == 4:
                    newton(1, n + 1)
                    for h in range(HF):
                        last = v.tensor_scalar(fv[:, h, :], fd[:, h, :], rs[1][:, h:h + 1], None, ALU.mult)
                    last.then_inc(fc1_in, 1)
                if u == 5:
                    v.wait_ge(fc1_out, n + 1)
                    v.tensor_scalar(hr[:, :], SA[0:RED, 0, 8:10], 0.0, None, ALU.max)
                    v.drain()
                    v.tensor_tensor(hs[:, :], hr[:, 0:1], hr[:, 1:2], ALU.add).then_inc(fc2_in, 1)
                if u == 6:
                    v.wait_ge(fc2_out, n + 1)
                    v.tensor_scalar(garg[:, :], SA[:, 0, 10:12], CLAMP, None, ALU.max).then_inc(gate_arg, 1)
                if u == 7:
                    v.wait_ge(gate_exp, n + 1)
                    v.tensor_scalar(gden[:, :], gexp[:, :], 1.0, None, ALU.add)
                    v.drain()
                    v.reciprocal(gate[:, :], gden[:, :])
                    v.drain()
                    v.tensor_tensor(kcur[:, :], gate[:, :], rs[1][:, :], ALU.mult)
                    v.drain()
                    v.scalar_tensor_tensor(nb[:, :], gm[1][:, :], -1.0, kcur[:, :], ALU.mult, ALU.mult).then_inc(gate_done, 1)
                    v.tensor_copy(kA[:, n, :], kcur[:, :])
                if GATE0 <= u < GATE0 + CH:
                    pair(n, u - GATE0)
                if GATE0 < u <= GATE0 + CH:
                    max_pixels(n, u - GATE0 - 1)

            def stage_next_small(n, u):
                if u == 5:
                    gn_aggregate(0)
                if u == 7:
                    gn_deviation(0, n + 1)
                if u == 8:
                    gn_variance(0, n + 1)
                if u == 9:
                    newton(0, n + 1)

            def stage_next(n, u):
                if u == 3:
                    x_stats(n, range(CH // 2))
                if u == 4:
                    x_stats(n, range(CH // 2, CH))
                for c in PREP.get(u, []):
                    prep(n, c)
                    low(n, c)

            def work(i, live):
                for u in range(UN):
                    if u == 0 and live.conv:
                        for c in PREP_OWN:
                            prep(i, c)
                            low(i, c)
                    if live.next:
                        stage_next_small(i + 1, u)
                    if live.b:
                        stage_b(i - 2, u)
                    if live.a:
                        stage_a(i - 1, u)
                    if live.next:
                        stage_next(i + 1, u)
                    if live.conv and u > 0 and u % 2 == 0:
                        x1_stats(i, u // 2 - 1)

            iterations(v, NB, work)

            v.drain()
            v.tensor_tensor(bm[:, :, :], mwA[:, :, :, 0], kA[:, :, :], ALU.mult)
            v.tensor_tensor(bq[:, :, :], mwA[:, :, :, 1], kA[:, :, :], ALU.mult)
            v.drain()
            v.tensor_tensor(bq[:, :, :], bq[:, :, :], kA[:, :, :], ALU.mult)
            v.tensor_reduce(bs[:, :], bm[:, :, :].rearrange("p n h -> p h n"), AX_X, ALU.add)
            v.drain()
            v.tensor_scalar(bmean[:, :], bs[:, :], 1.0 / NB, None, ALU.mult)
            v.drain()
            for h in range(HF):
                v.tensor_scalar(bm[:, :, h], bm[:, :, h], bmean[:, h:h + 1], None, ALU.subtract)
            v.drain()
            v.tensor_tensor(bm[:, :, :], bm[:, :, :], bm[:, :, :], ALU.mult)
            v.drain()
            v.tensor_tensor(bq[:, :, :], bq[:, :, :], bm[:, :, :], ALU.add)
            v.drain()
            v.tensor_reduce(bs[:, :], bq[:, :, :].rearrange("p n h -> p h n"), AX_X, ALU.add)
            v.drain()
            v.tensor_scalar(vv[2][:, :], bs[:, :], 1.0 / NB, 1e-5, ALU.mult, ALU.add).then_inc(v_ready[2], 1)
            newton(2, 1)
            v.tensor_tensor(bscale[:, :], rs[2][:, :], bnp[:, 0, :], ALU.mult)
            v.drain()
            for h in range(HF):
                v.tensor_scalar(bA[:, :, h], kA[:, :, h], bscale[:, h:h + 1], None, ALU.mult)
            v.tensor_tensor(bs[:, :], bmean[:, :], bscale[:, :], ALU.mult)
            v.drain()
            v.tensor_tensor(bB[:, :], bnp[:, 1, :], bs[:, :], ALU.subtract).then_inc(bn_ready, 1)

            def product(t, s, c2, h, n):
                k = N2 * t + HF * c2 + h
                if h == 0:
                    v.wait_ge(spread, (CH // 2) * t + c2 + 1)
                wait(v, add_pool if h else add_dve, (k - RING2 - h) // 2 + 1 if isinstance(k, int) else
                     (N2 // 2) * t + c2 - RING2 // 2 + 1)
                buf = step_buf((N2 * s + HF * c2 + h) % RING2)
                pair_ = cv[:, 2 * (c2 % 2):2 * (c2 % 2) + 2, 0:CW]
                v.wait_ge(bn_ready, 1)
                v.scalar_tensor_tensor(buf.rearrange("p (e c) -> p e c", e=2),
                                       chunk(s, h, 2 * c2, 2).rearrange("p (e c) -> p e c", e=2),
                                       gmA[:, n, h:h + 1], pair_, ALU.subtract, ALU.mult).then_inc(prod_done, 1)

            def add(t, s, c2):
                k = N2 * t + HF * c2
                v.wait_ge(act_done, k + 1)
                at = chunk(s, 0, 2 * c2, 2)
                v.tensor_tensor(at, at, step_buf((N2 * s + HF * c2) % RING2), ALU.add).then_inc(add_dve, 1)

            def phase2(t, s, n, back):
                if back is not None:
                    v.wait_ge(x1_back[s], back)
                v.tensor_copy(bAs[:, s, :], bA[:, n, :])
                for c2 in range(CH // 2):
                    product(t, s, c2, 0, n)
                    product(t, s, c2, 1, n)
                    if c2 > 0:
                        add(t, s, c2 - 1)
                add(t, s, CH // 2 - 1)

            for s in range(SLOTS):
                phase2(s, s, NB - SLOTS + s, None)
            with v.Fori(1, NB // SLOTS) as q:
                for s in range(SLOTS):
                    phase2(SLOTS * q + s, s, SLOTS * (q - 1) + s, 16 * q)


def kernel(**inputs):
    import numpy as np
    import concourse.bacc as bacc
    from concourse.bass_utils import run_bass_kernel_spmd

    x = np.asarray(inputs["x"])
    n = x.shape[0]
    halves = lambda a: np.ascontiguousarray(np.asarray(a).reshape(2, P).T)
    by_state = lambda a: np.repeat(np.asarray(a).reshape(-1), CH)
    every = lambda a: np.repeat(np.asarray(a).reshape(-1), P)
    w1 = np.asarray(inputs["L1_conv_ca_w1"])
    arrays = {
        "x": np.ascontiguousarray(x.reshape(n, PX, 2, P).transpose(0, 2, 3, 1)),
        "w": np.ascontiguousarray(np.asarray(inputs["L0_conv_W"]).reshape(TAPS * 2, P, 2 * P)),
        "bias": halves(inputs["L0_conv_b"]),
        "w1": np.ascontiguousarray(w1.T.reshape(2, P, RED).transpose(1, 0, 2)),
        "w2": np.ascontiguousarray(np.asarray(inputs["L1_conv_ca_w2"]).T),
        "lsa": np.ascontiguousarray(np.asarray(inputs["L1_conv_lsa_w"]).reshape(-1)),
        "scal": np.ascontiguousarray(np.stack(
            [by_state(inputs["L1_conv_A"]), by_state(inputs["L1_conv_B_w"]), by_state(inputs["L1_conv_B_b"]),
             by_state(inputs["L1_conv_C_w"]), by_state(inputs["L1_conv_C_b"]),
             every(inputs["L1_conv_d_w"]), every(inputs["L1_conv_d_b"])], axis=1)),
        "bn": np.ascontiguousarray(np.stack([halves(inputs["L1_conv_bn_gamma"]), halves(inputs["L1_conv_bn_beta"])], axis=1)),
    }
    nc = bacc.Bacc("TRN2", target_bir_lowering=False, num_devices=1)
    args = [nc.dram_tensor(f"in_{k}", a.shape, F32, kind="ExternalInput").ap() for k, a in arrays.items()]
    out = nc.dram_tensor("out", (n, 2, P, PX), F32, kind="ExternalOutput").ap()
    by_name = dict(zip(arrays, args))
    build_kernel(nc, by_name["x"], by_name["w"], by_name["bias"], by_name["w1"], by_name["w2"], by_name["lsa"],
                 by_name["scal"], by_name["bn"], out)
    r = run_bass_kernel_spmd(nc, [{f"in_{k}": a for k, a in arrays.items()}], core_ids=[0])
    got = r.results[0]["out"]
    return np.ascontiguousarray(got.reshape(n, 2, P, PX).transpose(0, 3, 1, 2).reshape(n, H, W, 2 * P))
```

```python
from contextlib import ExitStack

import concourse.bass as bass
from concourse import mybir

F32 = mybir.dt.float32
F16 = mybir.dt.float16
I32 = mybir.dt.int32
ALU = mybir.AluOpType
ACT = mybir.ActivationFunctionType
AX_X = mybir.AxisListType.X

P = 128
HF = 2
H = W = 56
PX = H * W
CH = 8
R = H // CH
CW = R * W
UN = CH * HF
SQ = 32
GC = 7
GW = PX // GC
GB = GW // SQ
NQ = PX // SQ
TAPS = 9
ST = 16
RED = 16
GS = 8
K7 = 7
PAD7 = K7 // 2
BAND = 2 * H - 1
MAXROW = 64
SLOTS = 4
CLAMP = -80.0

PREP = {9: [0], 10: [1, 2], 11: [3], 12: [4], 14: [5]}
PREP_OWN = [6, 7]
WSTAT = {9: [0], 10: [1], 11: [2], 12: [3], 13: [4], 14: [5], 15: [6, 7]}
GATE0 = 7


class Live:

    def __init__(self, i, n_images):
        self.conv = 0 <= i < n_images
        self.next = 0 <= i + 1 < n_images
        self.a = 0 <= i - 1 < n_images
        self.b = 0 <= i - 2 < n_images


def iterations(eng, n_images, work):
    full = Live(2, 4)
    for i in range(-1, 2):
        work(i, Live(i, n_images))
    with eng.Fori(2, n_images - 1) as i:
        work(i, full)
    for i in range(n_images - 1, n_images + 2):
        work(i, Live(i, n_images))


def wait(eng, sem, value):
    if not isinstance(value, int) or value > 0:
        eng.wait_ge(sem, value)


def build_kernel(nc, x, w, bias, w1, w2, lsa, scal, bn, out):
    NB = x.shape[0]
    assert NB % SLOTS == 0 and NB >= 4
    NPIX = float(NB * PX)
    WCOLS = TAPS * HF * 2 * P

    ctx = ExitStack()
    with ctx:
        def sb(name, shape, dt=F32):
            return ctx.enter_context(nc.sbuf_tensor(name, shape, dt))

        def bank(name, n=1):
            return ctx.enter_context(nc.psum_tensor(name, [P, n, 512], F32))

        def sem(name):
            return ctx.enter_context(nc.semaphore(name))

        x1_dram = nc.dram_tensor("x1_dram", (NB, HF, P, PX), F32, kind="Internal").ap()
        feat_dram = nc.dram_tensor("feat_dram", (2, PX), F32, kind="Internal").ap()
        g_dram = nc.dram_tensor("g_dram", (NB, PX), F32, kind="Internal").ap()
        band_dram = nc.dram_tensor("band_dram", (P, K7, BAND), F32, kind="Internal").ap()

        xs = sb("xs", [P, SLOTS, HF, PX])
        hl = sb("hl", [P, 2, HF, H + 2, W + 2], F16)
        tern = sb("tern", [P, TAPS, HF, 2 * P], F16)
        xn = sb("xn", [P, 2, HF, CW])
        rl = sb("rl", [P, 4, CW])
        xc = sb("xc", [P, 2, HF, GW])
        xp = sb("xp", [P, 2, GW])
        xt = sb("xt", [P, 2, GW])
        wk = sb("wk", [P, 2, HF, CW])
        gB = sb("gB", [P, PX])

        ident = sb("ident", [P, P])
        ones = sb("ones", [P, P])
        gmat = sb("gmat", [P, P])
        selr = sb("selr", [P, R, H])
        lw = sb("lw", [P, K7, K7, 2])
        band = gB[:, 0:K7 * BAND].rearrange("p (a b) -> p a b", b=BAND)
        toep = sb("toep", [P, K7, H])
        rmask = sb("rmask", [1, P])
        pidx = sb("pidx", [P, 1], I32)
        pj = sb("pj", [P, 1], I32)
        pjf = sb("pjf", [P, 1])
        tgt = sb("tgt", [P, R])
        iot = sb("iot", [P, H])

        w1T = sb("w1T", [P, HF, RED])
        w2T = sb("w2T", [RED, HF * P])
        biasc = sb("biasc", [P, HF])
        sv = sb("sv", [P, 7])
        bnp = sb("bnp", [P, 2, HF])
        wred = sb("wred", [P, TAPS * HF])
        wstat = sb("wstat", [P, 8])
        alpha = sb("alpha", [P, 1])
        tick = sb("tick", [1, 1])

        st = [sb(f"st{q}", [P, HF, CH, 6]) for q in range(2)]
        stw = sb("stw", [P, HF, CH, 6])
        mv = [sb(f"mv{q}", [P, HF, 2]) for q in range(2)]
        gm = [sb(f"gm{q}", [P, HF]) for q in range(2)]
        dv = [sb(f"dv{q}", [P, HF]) for q in range(2)]
        dq = [sb(f"dq{q}", [P, HF]) for q in range(2)]
        vv = [sb(f"vv{q}", [P, HF]) for q in range(3)]
        lnv = [sb(f"lnv{q}", [P, HF]) for q in range(3)]
        r0 = [sb(f"r0{q}", [P, HF]) for q in range(3)]
        nt = [sb(f"nt{q}", [P, HF]) for q in range(3)]
        rs = [sb(f"rs{q}", [P, HF]) for q in range(3)]
        mx1 = sb("mx1", [P, CH, HF])
        fmx = sb("fmx", [P, HF])
        fd = sb("fd", [P, HF, 2])
        fv = sb("fv", [P, HF, 2])
        hr = sb("hr", [RED, 2])
        hs = sb("hs", [RED, 1])
        garg = sb("garg", [P, HF])
        gexp = sb("gexp", [P, HF])
        gden = sb("gden", [P, HF])
        gate = sb("gate", [P, HF])
        kcur = sb("kcur", [P, HF])
        nb = sb("nb", [P, HF])
        nbx = sb("nbx", [P, HF])
        red = sb("red", [P, 2, NQ])
        maps = sb("maps", [NQ, 2, SQ])
        feat = sb("feat", [P, W + 2 * PAD7])

        ms = sb("ms", [P, CW])
        zs = sb("zs", [P, CW])
        nz = sb("nz", [P, CW])
        es = sb("es", [P, CW])
        us = sb("us", [P, CW])
        ls = sb("ls", [P, CW])
        de = sb("de", [P, CW])
        dA = sb("dA", [P, CW])
        sumd = sb("sumd", [P, 1])
        pe_ = sb("pend", [P, 1])
        rp = sb("rp", [1, P])
        rh = sb("rh", [1, P])
        rH = sb("rH", [1, P])
        hin = sb("hin", [1, P])
        hinc = sb("hinc", [P, 1])
        sy = sb("sy", [H, 2, W])
        sye = sb("sye", [H, 2, W])
        syd = sb("syd", [H, 2, W])
        syr = sb("syr", [H, 2, W])
        g56 = sb("g56", [H, W])
        mwt = sb("mwt", [P, HF, 2])

        gmA = sb("gmA", [P, NB, HF])
        kA = sb("kA", [P, NB, HF])
        mwA = sb("mwA", [P, NB, HF, 2])
        bm = sb("bm", [P, NB, HF])
        bq = sb("bq", [P, NB, HF])
        bs = sb("bs", [P, HF])
        bmean = sb("bmean", [P, HF])
        bscale = sb("bscale", [P, HF])
        bA = sb("bA", [P, NB, HF])
        bAs = sb("bAs", [P, SLOTS, HF])
        bB = sb("bB", [P, HF])

        cv = bank("cv", 4)
        Mb = bank("Mb")
        TR = bank("TR")
        SA = bank("SA")
        SB = bank("SB")
        S7 = Mb[0:H, 0, 0:W]
        TRv = TR[0:NQ, 0, 0:2 * P].rearrange("p (a q i) -> p a i q", a=2, i=SQ)
        ROWP = SB[0:1, 0, 128:256]
        ROWH = SB[0:1, 0, 256:384]
        HIN = SB[:, 0, 384:385]
        Y56 = SB[0:H, 0, 400:400 + W]

        params = sem("params"); w_loaded = sem("w_loaded"); lw_loaded = sem("lw_loaded")
        pool_const = sem("pool_const"); pool_zero = sem("pool_zero"); wa_ready = sem("wa_ready"); dve_const = sem("dve_const")
        w_sum = sem("w_sum"); w_tot = sem("w_tot"); w_cnt = sem("w_cnt"); w_cnt_tot = sem("w_cnt_tot")
        w_ready = sem("w_ready"); tern_ready = sem("tern_ready"); band_ready = sem("band_ready"); band_stored = sem("band_stored")
        toep_ready = sem("toep_ready")
        x_loaded = sem("x_loaded"); x1_stored = sem("x1_stored")
        norm_ready = sem("norm_ready"); hi_done = sem("hi_done"); lo_done = sem("lo_done")
        conv_done = sem("conv_done"); relu_done = sem("relu_done"); x1_done = sem("x1_done")
        mean_in = [sem(f"mean_in{q}") for q in range(2)]
        mean_out = [sem(f"mean_out{q}") for q in range(2)]
        var_in = [sem(f"var_in{q}") for q in range(2)]
        var_out = [sem(f"var_out{q}") for q in range(2)]
        v_ready = [sem(f"v_ready{q}") for q in range(3)]
        rs_guess = [sem(f"rs_guess{q}") for q in range(3)]
        fc1_in = sem("fc1_in"); fc1_out = sem("fc1_out"); fc2_in = sem("fc2_in"); fc2_out = sem("fc2_out")
        gate_arg = sem("gate_arg"); gate_exp = sem("gate_exp"); gate_done = sem("gate_done")
        xc_done = sem("xc_done"); pair_sum_done = sem("pair_sum_done"); pair_max_done = sem("pair_max_done"); turned = sem("turned")
        red_ready = sem("red_ready"); red_turned = sem("red_turned"); maps_ready = sem("maps_ready")
        maps_stored = sem("maps_stored"); ms_loaded = sem("ms_loaded"); ms_read = sem("ms_read")
        nz_ready = sem("nz_ready"); e_ready = sem("e_ready"); u_ready = sem("u_ready"); l_ready = sem("l_ready")
        delta_ready = sem("delta_ready"); decay_ready = sem("decay_ready"); ends_ready = sem("ends_ready")
        rows_out = sem("rows_out"); hin_ready = sem("hin_ready"); hin_out = sem("hin_out")
        hc_ready = sem("hc_ready"); y_done = sem("y_done"); c7_done = sem("c7_done"); s_taken = sem("s_taken")
        sy_ready = sem("sy_ready"); sye_ready = sem("sye_ready"); g_ready = sem("g_ready")
        feat_loaded = sem("feat_loaded")
        g_stored = sem("g_stored"); g_spread = sem("g_spread"); w_done = sem("w_done")
        bn_ready = sem("bn_ready"); grow_loaded = [sem(f"grow_loaded{k}") for k in range(2)]
        x1_back = [sem(f"x1_back{k}") for k in range(SLOTS)]
        out_stored = [sem(f"out_stored{k}") for k in range(SLOTS)]
        spread = sem("spread"); prod_done = sem("prod_done"); act_done = sem("act_done")
        add_dve = sem("add_dve"); add_pool = sem("add_pool")

        C2 = 2 * CW
        N2 = CH // 2 * HF
        RING2 = 4
        ring2 = [xn[:, :, :, :].rearrange("p a h c -> p (a h c)"), xc[:, :, :, :].rearrange("p a h c -> p (a h c)")]
        growt = gB

        wj, wv, wa = (xs[:, k, :, :].rearrange("p h x -> p (h x)")[:, 0:WCOLS] for k in (1, 2, 3))

        def chunk(slot, h, c, n=1):
            return xs[:, slot, h, c * CW:(c + n) * CW]

        def rows(ap):
            return ap.rearrange("p (r w) -> p r w", w=W)

        def step_buf(k):
            return ring2[k // 2][:, (k % 2) * C2:(k % 2) * C2 + C2]

        block = ctx.enter_context(nc.Block())

        @block.sync
        def _(sp):
            sp.dma_start(wv.rearrange("p (t m) -> p t m", m=2 * P),
                         w.rearrange("t p m -> p t m")).then_inc(w_loaded, 16)
            sp.dma_start(biasc[:, :], bias).then_inc(params, 16)
            sp.dma_start(w1T[:, :, :], w1).then_inc(params, 16)
            sp.dma_start(w2T[:, :], w2).then_inc(params, 16)
            sp.dma_start(sv[:, :], scal).then_inc(params, 16)
            sp.dma_start(bnp[:, :, :], bn).then_inc(params, 16)
            sp.dma_start(lw[:, :, :, :].rearrange("p a b c -> p (a b c)"), lsa.partition_broadcast(P)).then_inc(lw_loaded, 16)
            sp.wait_ge(band_ready, 1)
            sp.dma_start(band_dram, band).then_inc(band_stored, 16)
            sp.wait_ge(band_stored, 16)
            for c in range(2):
                src = bass.AP(tensor=band_dram.tensor, offset=c * MAXROW * K7 * BAND + H - 1,
                              ap=[[K7 * BAND - 1, H], [BAND, K7], [1, H]])
                sp.dma_start(toep[c * MAXROW:c * MAXROW + H, :, :], src).then_inc(toep_ready, 16)

            def work(i, live):
                if live.next:
                    n = i + 1
                    if not isinstance(i, int) or i >= 2:
                        sp.wait_ge(x1_stored, 16 * (i - 1))
                        sp.wait_ge(ms_read, i - 1)
                    elif i == 0:
                        sp.wait_ge(w_ready, 1)
                    wait(sp, x_loaded, 16 * n)
                    sp.dma_start(xs[:, n % SLOTS, :, :], x[n].rearrange("h p x -> p h x")).then_inc(x_loaded, 16)
                if live.a:
                    sp.wait_ge(x1_done, UN * i)
                    wait(sp, x1_stored, 16 * (i - 1))
                    sp.dma_start(x1_dram[i - 1].rearrange("h p x -> p h x"),
                                 xs[:, (i - 1) % SLOTS, :, :]).then_inc(x1_stored, 16)
                if live.b:
                    n = i - 2
                    sp.wait_ge(g_ready, n + 1)
                    sp.dma_start(g_dram[n].rearrange("(a b) -> a b", b=W), g56[:, :]).then_inc(g_stored, 16)
                    sp.wait_ge(g_stored, 16 * (n + 1))
                    sp.dma_start(gB[:, :], g_dram[n].partition_broadcast(P)).then_inc(g_spread, 16)
                if live.a:
                    n = i - 1
                    sp.wait_ge(maps_ready, n + 1)
                    sp.dma_start(feat_dram.rearrange("c (b x) -> b c x", x=SQ), maps[:, :, :]).then_inc(maps_stored, 16)
                    if live.b:
                        sp.wait_ge(hc_ready, i - 1)
                        sp.wait_ge(c7_done, i - 1)
                    sp.wait_ge(maps_stored, 16 * (n + 1))
                    sp.dma_start(ms[:, :], bass.AP(tensor=feat_dram.tensor, offset=0,
                                                   ap=[[0, ST], [CW, CH], [1, CW]])).then_inc(ms_loaded, 16)
                    for c in range(2):
                        sp.dma_start(feat[c * MAXROW:c * MAXROW + H, PAD7:PAD7 + W],
                                     feat_dram[c].rearrange("(a b) -> a b", b=W)).then_inc(feat_loaded, 16)

            iterations(sp, NB, work)

            sp.wait_ge(x1_stored, 16 * NB)
            sp.wait_ge(w_done, CH * NB)

            def grow(n, k):
                sp.dma_start(growt[32 * k:32 * k + 1, :], g_dram[n].rearrange("(a b) -> a b", a=1)).then_inc(grow_loaded[k], 16)

            def finish(t, s, n):
                for part in range(2):
                    done = (t * 2 + part + 1) * (CH // 4)
                    cols = slice(part * PX // 2, (part + 1) * PX // 2)
                    sp.wait_ge(add_dve, done)
                    sp.wait_ge(add_pool, done)
                    sp.dma_start(out[n, :, :, cols].rearrange("h p x -> p h x"), xs[:, s, :, cols]).then_inc(out_stored[s], 16)

            def refill(s, n, count):
                sp.wait_ge(out_stored[s], 32 * count)
                sp.dma_start(xs[:, s, :, :], x1_dram[n].rearrange("h p x -> p h x")).then_inc(x1_back[s], 16)

            for k in range(2):
                grow(NB - SLOTS + k, k)
            for s in range(SLOTS):
                finish(s, s, NB - SLOTS + s)
                grow((NB - SLOTS + s + 2) % NB, s % 2)
                if s > 0:
                    refill(s - 1, s - 1, 1)

            def middle(q):
                for s in range(SLOTS):
                    n = SLOTS * (q - 1) + s
                    finish(SLOTS * q + s, s, n)
                    grow(n + 2, s % 2)
                    refill((s - 1) % SLOTS, n + SLOTS - 1, q + 1 if s > 0 else q)

            if NB // SLOTS > 2:
                with sp.Fori(1, NB // SLOTS - 1) as q:
                    middle(q)
            for s in range(SLOTS):
                n = NB - 2 * SLOTS + s
                finish(NB - SLOTS + s, s, n)
                if s < 2:
                    grow(n + 2, s)
                if s == 0:
                    refill(SLOTS - 1, n + SLOTS - 1, NB // SLOTS - 1)
            for s in range(SLOTS):
                sp.wait_ge(out_stored[s], 32 * (NB // SLOTS))

        @block.gpsimd
        def _(pool):
            pool.memset(ident[:, :], 0.0).then_inc(pool_const, 1)
            pool.memset(gmat[:, :], 1.0 / GS).then_inc(pool_const, 1)
            pool.memset(ones[:, :], 1.0).then_inc(pool_const, 1)
            pool.memset(band, 0.0).then_inc(pool_zero, 1)
            border = hl[:, :, :, :, :].rearrange("p a h r c -> p (a h r) c")
            pool.memset(border[:, :, 0:1], 0.0).then_inc(pool_zero, 1)
            pool.memset(border[:, :, W + 1:W + 2], 0.0).then_inc(pool_zero, 1)
            pool.memset(feat[:, :], 0.0).then_inc(pool_zero, 1)
            pool.memset(toep[:, :, :], 0.0).then_inc(pool_zero, 1)
            pool.memset(hin[:, :], 0.0).then_inc(pool_zero, 1)
            pool.iota(pidx[:, :], pattern=[[0, 1]], base=0, channel_multiplier=1).then_inc(pool_const, 1)
            pool.iota(iot[:, :], pattern=[[1, H]], base=0, channel_multiplier=0,
                      allow_small_or_imprecise_dtypes=True).then_inc(pool_const, 1)
            pool.wait_ge(pool_const, 5)
            pool.affine_select(out=ident[:, :], in_=ident[:, :], compare_op=ALU.not_equal, fill=1.0, base=0,
                               pattern=[[-1, P]], channel_multiplier=1).then_inc(pool_const, 1)
            g3 = gmat[:, :].rearrange("p (a b) -> p a b", b=GS)
            pool.affine_select(out=g3, in_=g3, compare_op=ALU.is_ge, fill=0.0, base=0,
                               pattern=[[-GS, P // GS], [0, GS]], channel_multiplier=1).then_inc(pool_const, 1)
            pool.wait_ge(pool_const, 7)
            pool.affine_select(out=g3, in_=g3, compare_op=ALU.is_ge, fill=0.0, base=GS - 1,
                               pattern=[[GS, P // GS], [0, GS]], channel_multiplier=-1).then_inc(pool_const, 1)

            def residual(n, u):
                b, o = divmod(u, HF)
                pool.wait_ge(relu_done, UN * n + u + 1)
                pool.wait_ge(w_ready, 1)
                at = chunk(n % SLOTS, o, b)
                pool.tensor_tensor(at, at, rl[:, u % 4, :], ALU.add).then_inc(x1_done, 1)

            def low(n, c):
                pool.wait_ge(hi_done, CH * n + c + 1)
                rows_ = slice(1 + R * c, 1 + R * (c + 1))
                for h in range(HF):
                    last = pool.tensor_tensor(hl[:, 1, h, rows_, 1:1 + W], rows(xn[:, c % 2, h, :]),
                                              hl[:, 0, h, rows_, 1:1 + W], ALU.subtract)
                last.then_inc(lo_done, 1)

            def pair_sum(n, c):
                pool.wait_ge(xc_done, GC * n + c + 1)
                wait(pool, turned, GC * n + c)
                pool.tensor_tensor(xp[:, 0, :], xc[:, c % 2, 0, :], xc[:, c % 2, 1, :], ALU.add).then_inc(pair_sum_done, 1)

            def work(i, live):
                for u in range(UN):
                    if u == 0 and live.conv:
                        for c in PREP_OWN:
                            if c == PREP_OWN[0] and live.a:
                                residual(i - 1, UN - 1)
                            low(i, c)
                    elif u == 0 and live.a:
                        residual(i - 1, UN - 1)
                    if u > 0 and live.conv:
                        residual(i, u - 1)
                    if live.a and GATE0 <= u < GATE0 + GC:
                        pair_sum(i - 1, u - GATE0)
                    if live.next:
                        for c in PREP.get(u, []):
                            low(i + 1, c)

            iterations(pool, NB, work)

            def add2(t, s, c2, h):
                k = N2 * t + HF * c2 + h
                pool.wait_ge(act_done, k + 1)
                at = chunk(s, h, 2 * c2, 2)
                pool.tensor_tensor(at, at, step_buf(k_static(s, c2, h)), ALU.add).then_inc(add_pool, 1)

            def k_static(s, c2, h):
                return (N2 * s + HF * c2 + h) % RING2

            def phase2(t, s):
                for c2 in range(CH // 2):
                    add2(t, s, c2, 1)

            for s in range(SLOTS):
                phase2(s, s)
            with pool.Fori(1, NB // SLOTS) as q:
                for s in range(SLOTS):
                    phase2(SLOTS * q + s, s)

        @block.scalar
        def _(act):
            def relu(n, u):
                b, o = divmod(u, HF)
                act.wait_ge(conv_done, UN * n + u + 1)
                wait(act, x1_done, UN * n + u - 3)
                act.wait_ge(w_ready, 1)
                act.activation(rl[:, u % 4, :], cv[:, u % 4, 0:CW], ACT.Relu, bias=biasc[:, o:o + 1],
                               scale=alpha[:, 0:1]).then_inc(relu_done, 1)

            def high(n, c):
                act.wait_ge(norm_ready, n + 1)
                wait(act, lo_done, CH * n + c - 1)
                act.wait_ge(pool_zero, 6)
                for h in range(HF):
                    act.activation(xn[:, c % 2, h, :], chunk(n % SLOTS, h, c), ACT.Identity,
                                   bias=nbx[:, h:h + 1], scale=rs[0][:, h:h + 1])
                act.drain()
                wait(act, conv_done, UN * (n - 1) + 2 * min(c + 1, CH - 1) + 2)
                act.wait_ge(pool_zero, 6)
                act.copy(hl[:, 0, :, 1 + R * c:1 + R * (c + 1), 1:1 + W],
                         xn[:, c % 2, :, :].rearrange("p h (r w) -> p h r w", w=W)).then_inc(hi_done, 1)

            def rsqrt_guess(q, count):
                act.wait_ge(v_ready[q], count)
                act.activation(lnv[q][:, :], vv[q][:, :], ACT.Ln)
                act.drain()
                act.activation(r0[q][:, :], lnv[q][:, :], ACT.Exp, scale=-0.5).then_inc(rs_guess[q], 1)

            def gated(n, c):
                act.wait_ge(gate_done, n + 1)
                wait(act, pair_sum_done, GC * n + c - 1)
                wait(act, pair_max_done, GC * n + c - 1)
                act.wait_ge(w_ready, 1)
                for h in range(HF):
                    last = act.activation(xc[:, c % 2, h, :], xs[:, n % SLOTS, h, c * GW:(c + 1) * GW], ACT.Identity,
                                          bias=nb[:, h:h + 1], scale=kcur[:, h:h + 1])
                last.then_inc(xc_done, 1)

            def work(i, live):
                for u in range(UN):
                    if u == 0 and live.conv:
                        for c in PREP_OWN:
                            if c == PREP_OWN[0] and live.a:
                                relu(i - 1, UN - 1)
                            high(i, c)
                    elif u == 0 and live.a:
                        relu(i - 1, UN - 1)
                    if u > 0 and live.conv:
                        relu(i, u - 1)
                    if live.b and u == 0:
                        act.wait_ge(nz_ready, i - 1)
                        act.activation(es[:, :], nz[:, :], ACT.Exp).then_inc(e_ready, 1)
                    if live.b and u == 1:
                        act.wait_ge(u_ready, i - 1)
                        act.activation(ls[:, :], us[:, :], ACT.Ln).then_inc(l_ready, 1)
                    if live.b and u == 2:
                        act.wait_ge(delta_ready, i - 1)
                        act.activation(dA[:, :], de[:, :], ACT.Exp, scale=sv[:, 0:1])
                        act.activation(pe_[:, :], sumd[:, :], ACT.Exp, scale=sv[:, 0:1]).then_inc(decay_ready, 1)
                    if live.a and u == 3:
                        rsqrt_guess(1, i)
                    if live.b and u == 6:
                        act.wait_ge(sy_ready, i - 1)
                        act.activation(sye[:, :, :], sy[:, :, :], ACT.Exp, scale=-1.0).then_inc(sye_ready, 1)
                    if live.a and u == 6:
                        act.wait_ge(gate_arg, i)
                        act.activation(gexp[:, :], garg[:, :], ACT.Exp, scale=-1.0).then_inc(gate_exp, 1)
                    if live.next and u == 8:
                        rsqrt_guess(0, i + 2)
                    if live.a and GATE0 <= u < GATE0 + GC:
                        gated(i - 1, u - GATE0)
                    if live.next:
                        for c in PREP.get(u, []):
                            high(i + 1, c)

            act.wait_ge(w_loaded, 16)
            act.activation(wa, wv, ACT.Abs).then_inc(wa_ready, 1)
            act.wait_ge(params, 5 * 16)
            iterations(act, NB, work)
            rsqrt_guess(2, 1)

            def phase2(t, s):
                for c2 in range(CH // 2):
                    for h in range(HF):
                        k = N2 * t + HF * c2 + h
                        act.wait_ge(prod_done, k + 1)
                        act.wait_ge(bn_ready, 1)
                        buf = step_buf((N2 * s + HF * c2 + h) % RING2)
                        act.activation(buf, buf, ACT.Relu, bias=bB[:, h:h + 1],
                                       scale=bAs[:, s, h:h + 1]).then_inc(act_done, 1)

            for s in range(SLOTS):
                phase2(s, s)
            with act.Fori(1, NB // SLOTS) as q:
                for s in range(SLOTS):
                    phase2(SLOTS * q + s, s)

        @block.tensor
        def _(pe):
            def conv(n, u):
                b, o = divmod(u, HF)
                wait(pe, relu_done, UN * n + u - 3)
                if o == 0:
                    pe.wait_ge(lo_done, CH * n + min(b + 1, CH - 1) + 1)
                order = [(k, dy, dx, part) for dy in (1, 0, 2) for k in range(HF) for dx in range(3) for part in range(2)]
                for at, (k, dy, dx, part) in enumerate(order):
                    ra = 1 if b == 0 and dy == 0 else 0
                    rb = R - 1 if b == CH - 1 and dy == 2 else R
                    last = pe.matmul(cv[:, u % 4, ra * W:rb * W], tern[:, 3 * dy + dx, k, o * P:(o + 1) * P],
                                     hl[:, part, k, R * b + dy + ra:R * b + dy + rb, dx:dx + W],
                                     start=(at == 0), stop=(at == len(order) - 1))
                last.then_inc(conv_done, 1)

            def group_mean(q, count):
                pe.wait_ge(mean_in[q], count)
                pe.matmul(SA[:, 0, 4 * q:4 * q + 2], gmat[:, :], mv[q][:, :, 0], start=True, stop=True).then_inc(mean_out[q], 1)

            def group_var(q, count):
                pe.wait_ge(var_in[q], count)
                pe.matmul(SA[:, 0, 4 * q + 2:4 * q + 4], gmat[:, :], dv[q][:, :], start=True, stop=True).then_inc(var_out[q], 1)

            def work(i, live):
                for u in range(UN):
                    if live.conv:
                        if isinstance(i, int) and i == 0 and u == 0:
                            pe.wait_ge(tern_ready, 1)
                        conv(i, u)
                    if isinstance(i, int) and i == 0 and u == 0:
                        pe.wait_ge(w_cnt, 1)
                        pe.matmul(SA[:, 0, 2:4], ones[:, :], wstat[:, 2:4], start=True, stop=True).then_inc(w_cnt_tot, 1)
                        pe.wait_ge(params, 5 * 16)
                        pe.wait_ge(dve_const, 1)
                        pe.wait_ge(toep_ready, 32)
                    if live.b:
                        n = i - 2
                        if u == 3:
                            pe.wait_ge(ends_ready, n + 1)
                            pe.matmul(ROWP, pe_[:, :], ident[:, :], start=True, stop=True)
                            pe.matmul(ROWH, nz[:, CW - 1:CW], ident[:, :], start=True, stop=True).then_inc(rows_out, 1)
                        if u == 4:
                            pe.wait_ge(feat_loaded, 32 * (n + 1))
                            for dx in range(K7):
                                last = pe.matmul(S7, toep[0:MAXROW + H, dx, :], feat[0:MAXROW + H, dx:dx + W],
                                                 start=(dx == 0), stop=(dx == K7 - 1))
                            last.then_inc(c7_done, 1)
                            pe.wait_ge(hin_ready, n + 1)
                            pe.matmul(HIN, hin[:, :], ones[0:1, 0:1], start=True, stop=True).then_inc(hin_out, 1)
                        if u == 5:
                            pe.wait_ge(hc_ready, n + 1)
                            for r in range(R):
                                last = pe.matmul(Y56, selr[:, r, :], es[:, r * W:(r + 1) * W],
                                                 start=(r == 0), stop=(r == R - 1))
                            last.then_inc(y_done, 1)
                    if live.a:
                        n = i - 1
                        if u == 1:
                            group_mean(1, n + 1)
                        if u == 2:
                            group_var(1, n + 1)
                        if u == 4:
                            pe.wait_ge(fc1_in, n + 1)
                            for h in range(HF):
                                last = pe.matmul(SA[0:RED, 0, 8:10], w1T[:, h, :], fv[:, h, :], start=(h == 0), stop=(h == 1))
                            last.then_inc(fc1_out, 1)
                        if u == 5:
                            pe.wait_ge(fc2_in, n + 1)
                            for h in range(HF):
                                last = pe.matmul(SA[:, 0, 10 + h:11 + h], w2T[:, h * P:(h + 1) * P], hs[:, :], start=True, stop=True)
                            last.then_inc(fc2_out, 1)
                        if u == GATE0 + GC:
                            pe.wait_ge(red_ready, n + 1)
                            for a in range(2):
                                last = pe.transpose(TR[0:NQ, 0, a * P:(a + 1) * P], red[:, a, :], ident[:, :])
                            last.then_inc(red_turned, 1)
                    if live.next:
                        if u == 6:
                            if live.a:
                                pe.wait_ge(gate_arg, i)
                            group_mean(0, i + 2)
                        if u == 7:
                            group_var(0, i + 2)

            pe.wait_ge(pool_const, 8)
            pe.wait_ge(w_sum, 1)
            pe.matmul(SA[:, 0, 0:1], ones[:, :], wstat[:, 0:1], start=True, stop=True).then_inc(w_tot, 1)
            iterations(pe, NB, work)

            def phase2(t, s, count):
                k = s % 2
                pe.wait_ge(grow_loaded[k], count)
                for c2 in range(CH // 2):
                    wait(pe, prod_done, N2 * t + HF * (c2 - 1))
                    for e in range(2):
                        last = pe.matmul(cv[:, 2 * (c2 % 2) + e, 0:CW], ones[32 * k:32 * k + 1, :],
                                         growt[32 * k:32 * k + 1, (2 * c2 + e) * CW:(2 * c2 + e + 1) * CW],
                                         start=True, stop=True)
                    last.then_inc(spread, 1)

            for s in range(SLOTS):
                phase2(s, s, 16 * (s // 2 + 1))
            with pe.Fori(1, NB // SLOTS) as q:
                for s in range(SLOTS):
                    phase2(SLOTS * q + s, s, 16 * (2 * q + s // 2 + 1))

        @block.vector
        def _(v):
            v.memset(rmask[:, :], 1.0)
            v.drain()
            v.memset(rmask[:, 0:P:CH], 0.0)
            v.wait_ge(lw_loaded, 16)
            v.wait_ge(pool_zero, 6)
            for c in range(2):
                a = c * MAXROW
                for dy in range(K7):
                    last = v.tensor_copy(band[a:a + H, :, H - 1 + PAD7 - dy], lw[a:a + H, dy, :, c])
            last.then_inc(band_ready, 1)
            v.wait_ge(pool_const, 8)
            v.tensor_scalar(pj[:, :], pidx[:, :], CH - 1, None, ALU.bitwise_and)
            v.drain()
            v.tensor_copy(pjf[:, :], pj[:, :])
            v.drain()
            for r in range(R):
                v.tensor_scalar(tgt[:, r:r + 1], pjf[:, :], float(R), float(r), ALU.mult, ALU.add)
            v.drain()
            for r in range(R):
                last = v.tensor_scalar(selr[:, r, :], iot[:, :], tgt[:, r:r + 1], None, ALU.is_equal)
            last.then_inc(dve_const, 1)
            v.wait_ge(w_loaded, 16)
            v.tensor_reduce(wred[:, :], wv.rearrange("p (a b) -> p a b", b=2 * P), AX_X, ALU.add, apply_absolute_value=True)
            v.drain()
            v.tensor_reduce(wstat[:, 0:1], wred[:, :], AX_X, ALU.add).then_inc(w_sum, 1)
            v.wait_ge(w_tot, 1)
            v.tensor_scalar(wstat[:, 1:2], SA[:, 0, 0:1], 1.0 / (WCOLS * P), 0.7, ALU.mult, ALU.mult)
            v.drain()
            v.tensor_scalar(wstat[:, 4:5], wstat[:, 1:2], -1.0, None, ALU.mult)
            v.drain()
            v.tensor_scalar(wj, wv, wstat[:, 4:5], None, ALU.is_le)
            v.drain()
            v.scalar_tensor_tensor(tern[:, :, :, :].rearrange("p t k m -> p (t k m)"), wv, wstat[:, 1:2], wj,
                                   ALU.is_ge, ALU.subtract).then_inc(tern_ready, 1)

            def count_kept():
                v.wait_ge(wa_ready, 1)
                v.drain()
                v.tensor_scalar(wj, wa, wstat[:, 1:2], None, ALU.is_gt, ALU.add, accum_out=wstat[:, 3:4])
                v.drain()
                v.scalar_tensor_tensor(wj, wa, wstat[:, 1:2], wa, ALU.is_gt, ALU.mult,
                                       accum_out=wstat[:, 2:3]).then_inc(w_cnt, 1)

            def scale_of_weights():
                v.wait_ge(w_cnt_tot, 1)
                v.tensor_copy(wstat[:, 5:7], SA[:, 0, 2:4])
                v.drain()
                v.reciprocal(wstat[:, 7:8], wstat[:, 6:7])
                v.drain()
                v.tensor_tensor(alpha[:, :], wstat[:, 5:6], wstat[:, 7:8], ALU.mult).then_inc(w_ready, 1)
                v.wait_ge(params, 5 * 16)

            def held(sem_, value):
                v.drain()
                v.wait_ge(sem_, value)
                v.memset(tick[:, :], 0.0)

            def x_stats(n, cs):
                held(x_loaded, 16 * (n + 1))
                for c in cs:
                    for h in range(HF):
                        v.bn_stats(st[0][:, h, c, :], chunk(n % SLOTS, h, c))

            def x1_stats(n, b):
                held(x1_done, UN * n + 2 * b + 2)
                for h in range(HF):
                    v.bn_stats(st[1][:, h, b, :], chunk(n % SLOTS, h, b))
                v.tensor_reduce(mx1[:, b, :], xs[:, n % SLOTS, :, b * CW:(b + 1) * CW], AX_X, ALU.max)

            def gn_aggregate(q):
                v.drain()
                for h in range(HF):
                    last = v.bn_aggr(mv[q][:, h, :], st[q][:, h, :, :].rearrange("p c s -> p (c s)"))
                last.then_inc(mean_in[q], 1)

            def gn_deviation(q, count):
                v.wait_ge(mean_out[q], count)
                v.tensor_copy(gm[q][:, :], SA[:, 0, 4 * q:4 * q + 2])
                v.drain()
                v.tensor_tensor(dq[q][:, :], mv[q][:, :, 0], gm[q][:, :], ALU.subtract)
                v.drain()
                v.tensor_tensor(dq[q][:, :], dq[q][:, :], dq[q][:, :], ALU.mult)
                v.drain()
                v.tensor_tensor(dv[q][:, :], dq[q][:, :], mv[q][:, :, 1], ALU.add).then_inc(var_in[q], 1)

            def gn_variance(q, count):
                v.wait_ge(var_out[q], count)
                v.tensor_scalar(vv[q][:, :], SA[:, 0, 4 * q + 2:4 * q + 4], 1e-5, None, ALU.add).then_inc(v_ready[q], 1)

            def newton(q, count):
                v.wait_ge(rs_guess[q], count)
                v.tensor_tensor(nt[q][:, :], r0[q][:, :], r0[q][:, :], ALU.mult)
                v.drain()
                v.tensor_tensor(nt[q][:, :], nt[q][:, :], vv[q][:, :], ALU.mult)
                v.drain()
                v.tensor_scalar(nt[q][:, :], nt[q][:, :], -0.5, 1.5, ALU.mult, ALU.add)
                v.drain()
                v.tensor_tensor(rs[q][:, :], r0[q][:, :], nt[q][:, :], ALU.mult)
                v.drain()

            def channels(n, c):
                v.wait_ge(xc_done, GC * n + c + 1)
                v.tensor_tensor(xp[:, 1, :], xc[:, c % 2, 0, :], xc[:, c % 2, 1, :], ALU.max).then_inc(pair_max_done, 1)
                v.drain()
                v.wait_ge(pair_sum_done, GC * n + c + 1)
                for a in range(2):
                    last = v.transpose(xt[:, a, :], xp[:, a, :])
                last.then_inc(turned, 1)
                v.drain()
                for a, op in enumerate((ALU.add, ALU.max)):
                    last = v.tensor_reduce(red[:, a, c * GB:(c + 1) * GB], xt[:, a, :].rearrange("p (b x) -> p b x", x=SQ),
                                           AX_X, op)
                if c == GC - 1:
                    last.then_inc(red_ready, 1)

            def channel_maps(n):
                v.wait_ge(red_turned, n + 1)
                if not isinstance(n, int) or n > 0:
                    v.wait_ge(maps_stored, 16 * n)
                v.tensor_reduce(maps[:, 0, :], TRv[:, 0, :, :], AX_X, ALU.add)
                v.tensor_reduce(maps[:, 1, :], TRv[:, 1, :, :], AX_X, ALU.max)
                v.drain()
                v.tensor_scalar(maps[:, 0, :], maps[:, 0, :], 1.0 / (HF * P), None, ALU.mult).then_inc(maps_ready, 1)

            def bn_chunk(n, c):
                if c == 0:
                    v.wait_ge(g_spread, 16 * (n + 1))
                for h in range(HF):
                    v.scalar_tensor_tensor(wk[:, c % 2, h, :], chunk(n % SLOTS, h, c), gmA[:, n, h:h + 1],
                                           gB[:, c * CW:(c + 1) * CW], ALU.subtract, ALU.mult)
                v.drain()
                for h in range(HF):
                    last = v.bn_stats(stw[:, h, c, :], wk[:, c % 2, h, :])
                last.then_inc(w_done, 1)
                if c == CH - 1:
                    v.drain()
                    for h in range(HF):
                        v.bn_aggr(mwt[:, h, :], stw[:, h, :, :].rearrange("p c s -> p (c s)"))
                    v.drain()
                    v.tensor_copy(mwA[:, n, :, :], mwt[:, :, :])

            def stage_b(n, u):
                if u == 0:
                    v.wait_ge(ms_loaded, 16 * (n + 1))
                    v.tensor_scalar(zs[:, :], ms[:, :], sv[:, 5:6], sv[:, 6:7], ALU.mult, ALU.add).then_inc(ms_read, 1)
                    v.drain()
                    v.scalar_tensor_tensor(nz[:, :], zs[:, :], -1.0, zs[:, :], ALU.mult, ALU.min).then_inc(nz_ready, 1)
                if u == 1:
                    v.wait_ge(e_ready, n + 1)
                    v.tensor_scalar(us[:, :], es[:, :], 1.0, None, ALU.add).then_inc(u_ready, 1)
                    v.drain()
                    v.scalar_tensor_tensor(de[:, :], us[:, :], 1.0, es[:, :], ALU.subtract, ALU.subtract)
                    v.drain()
                    v.scalar_tensor_tensor(zs[:, :], zs[:, :], 0.0, de[:, :], ALU.max, ALU.subtract)
                    v.drain()
                if u == 2:
                    v.wait_ge(l_ready, n + 1)
                    v.scalar_tensor_tensor(de[:, :], zs[:, :], 1.0, ls[:, :], ALU.mult, ALU.add,
                                           accum_out=sumd[:, :]).then_inc(delta_ready, 1)
                    v.tensor_scalar(us[:, :], ms[:, :], sv[:, 1:2], sv[:, 2:3], ALU.mult, ALU.add)
                    v.drain()
                    v.tensor_tensor(zs[:, :], de[:, :], ms[:, :], ALU.mult)
                    v.drain()
                    v.tensor_tensor(ls[:, :], zs[:, :], us[:, :], ALU.mult)
                    v.drain()
                if u == 3:
                    v.wait_ge(decay_ready, n + 1)
                    v.tensor_tensor_scan(nz[:, :], dA[:, :], ls[:, :], 0.0, ALU.mult, ALU.add).then_inc(ends_ready, 1)
                if u == 4:
                    v.wait_ge(rows_out, n + 1)
                    v.tensor_tensor(rp[:, :], ROWP, rmask[:, :], ALU.mult)
                    v.tensor_copy(rh[:, :], ROWH)
                    v.drain()
                    v.tensor_tensor_scan(rH[:, :], rp[:, :], rh[:, :], 0.0, ALU.mult, ALU.add)
                    v.drain()
                    v.tensor_tensor(hin[:, 1:P], rH[:, 0:P - 1], rmask[:, 1:P], ALU.mult).then_inc(hin_ready, 1)
                if u == 5:
                    v.wait_ge(c7_done, n + 1)
                    v.tensor_scalar(sy[:, 1, :], S7, CLAMP, None, ALU.max).then_inc(s_taken, 1)
                    v.tensor_scalar(us[:, :], ms[:, :], sv[:, 3:4], sv[:, 4:5], ALU.mult, ALU.add)
                    v.wait_ge(hin_out, n + 1)
                    v.tensor_copy(hinc[:, :], HIN)
                    v.drain()
                    v.tensor_tensor_scan(zs[:, :], dA[:, :], ls[:, :], hinc[:, 0:1], ALU.mult, ALU.add)
                    v.drain()
                    v.tensor_tensor(es[:, :], zs[:, :], us[:, :], ALU.mult).then_inc(hc_ready, 1)
                if u == 6:
                    v.wait_ge(y_done, n + 1)
                    v.tensor_scalar(sy[:, 0, :], Y56, CLAMP, None, ALU.max).then_inc(sy_ready, 1)
                if u == 7:
                    v.wait_ge(sye_ready, n + 1)
                    v.tensor_scalar(syd[:, :, :], sye[:, :, :], 1.0, None, ALU.add)
                    v.drain()
                    v.reciprocal(syr[:, :, :], syd[:, :, :])
                    v.drain()
                    v.tensor_tensor(g56[:, :], syr[:, 0, :], syr[:, 1, :], ALU.add).then_inc(g_ready, 1)
            def stage_a(n, u):
                if u == 0:
                    x1_stats(n, CH - 1)
                if u == 1:
                    gn_aggregate(1)
                if u == 2:
                    v.tensor_reduce(fmx[:, :], mx1[:, :, :].rearrange("p c h -> p h c"), AX_X, ALU.max)
                    gn_deviation(1, n + 1)
                if u == 3:
                    gn_variance(1, n + 1)
                    v.tensor_copy(gmA[:, n, :], gm[1][:, :])
                    v.tensor_tensor(fd[:, :, 0], mv[1][:, :, 0], gm[1][:, :], ALU.subtract)
                    v.tensor_tensor(fd[:, :, 1], fmx[:, :], gm[1][:, :], ALU.subtract)
                    v.drain()
                if u == 4:
                    newton(1, n + 1)
                    for h in range(HF):
                        last = v.tensor_scalar(fv[:, h, :], fd[:, h, :], rs[1][:, h:h + 1], None, ALU.mult)
                    last.then_inc(fc1_in, 1)
                if u == 5:
                    v.wait_ge(fc1_out, n + 1)
                    v.tensor_scalar(hr[:, :], SA[0:RED, 0, 8:10], 0.0, None, ALU.max)
                    v.drain()
                    v.tensor_tensor(hs[:, :], hr[:, 0:1], hr[:, 1:2], ALU.add).then_inc(fc2_in, 1)
                if u == 6:
                    v.wait_ge(fc2_out, n + 1)
                    v.tensor_scalar(garg[:, :], SA[:, 0, 10:12], CLAMP, None, ALU.max).then_inc(gate_arg, 1)
                if u == 7:
                    v.wait_ge(gate_exp, n + 1)
                    v.tensor_scalar(gden[:, :], gexp[:, :], 1.0, None, ALU.add)
                    v.drain()
                    v.reciprocal(gate[:, :], gden[:, :])
                    v.drain()
                    v.tensor_tensor(kcur[:, :], gate[:, :], rs[1][:, :], ALU.mult)
                    v.drain()
                    v.scalar_tensor_tensor(nb[:, :], gm[1][:, :], -1.0, kcur[:, :], ALU.mult, ALU.mult).then_inc(gate_done, 1)
                    v.tensor_copy(kA[:, n, :], kcur[:, :])
                if u == GATE0 + GC + 1:
                    channel_maps(n)

            def stage_next_small(n, u):
                if u == 5:
                    gn_aggregate(0)
                if u == 7:
                    gn_deviation(0, n + 1)
                if u == 8:
                    gn_variance(0, n + 1)
                if u == 9:
                    newton(0, n + 1)
                    v.scalar_tensor_tensor(nbx[:, :], gm[0][:, :], -1.0, rs[0][:, :], ALU.mult, ALU.mult).then_inc(norm_ready, 1)

            def stage_next(n, u):
                if u == 3:
                    x_stats(n, range(CH // 2))
                if u == 4:
                    x_stats(n, range(CH // 2, CH))
                if isinstance(n, int) and n == 0 and u == 10:
                    count_kept()

            def work(i, live):
                for u in range(UN):
                    if isinstance(i, int) and i == 0 and u == 0:
                        scale_of_weights()
                    if live.next:
                        stage_next_small(i + 1, u)
                    if live.b:
                        stage_b(i - 2, u)
                    if live.a:
                        stage_a(i - 1, u)
                    if live.next:
                        stage_next(i + 1, u)
                    if live.b:
                        for c in WSTAT.get(u, []):
                            bn_chunk(i - 2, c)
                    if live.conv and u > 0 and u % 2 == 0:
                        x1_stats(i, u // 2 - 1)
                    if live.a and GATE0 <= u < GATE0 + GC:
                        channels(i - 1, u - GATE0)

            iterations(v, NB, work)

            v.drain()
            v.tensor_tensor(bm[:, :, :], mwA[:, :, :, 0], kA[:, :, :], ALU.mult)
            v.tensor_tensor(bq[:, :, :], mwA[:, :, :, 1], kA[:, :, :], ALU.mult)
            v.drain()
            v.tensor_tensor(bq[:, :, :], bq[:, :, :], kA[:, :, :], ALU.mult)
            v.tensor_reduce(bs[:, :], bm[:, :, :].rearrange("p n h -> p h n"), AX_X, ALU.add)
            v.drain()
            v.tensor_scalar(bmean[:, :], bs[:, :], 1.0 / NB, None, ALU.mult)
            v.drain()
            for h in range(HF):
                v.tensor_scalar(bm[:, :, h], bm[:, :, h], bmean[:, h:h + 1], None, ALU.subtract)
            v.drain()
            v.tensor_tensor(bm[:, :, :], bm[:, :, :], bm[:, :, :], ALU.mult)
            v.drain()
            v.tensor_tensor(bq[:, :, :], bq[:, :, :], bm[:, :, :], ALU.add)
            v.drain()
            v.tensor_reduce(bs[:, :], bq[:, :, :].rearrange("p n h -> p h n"), AX_X, ALU.add)
            v.drain()
            v.tensor_scalar(vv[2][:, :], bs[:, :], 1.0 / NB, 1e-5, ALU.mult, ALU.add).then_inc(v_ready[2], 1)
            newton(2, 1)
            v.tensor_tensor(bscale[:, :], rs[2][:, :], bnp[:, 0, :], ALU.mult)
            v.drain()
            for h in range(HF):
                v.tensor_scalar(bA[:, :, h], kA[:, :, h], bscale[:, h:h + 1], None, ALU.mult)
            v.tensor_tensor(bs[:, :], bmean[:, :], bscale[:, :], ALU.mult)
            v.drain()
            v.tensor_tensor(bB[:, :], bnp[:, 1, :], bs[:, :], ALU.subtract).then_inc(bn_ready, 1)

            def product(t, s, c2, h, n):
                k = N2 * t + HF * c2 + h
                if h == 0:
                    v.wait_ge(spread, (CH // 2) * t + c2 + 1)
                wait(v, add_pool if h else add_dve, (k - RING2 - h) // 2 + 1 if isinstance(k, int) else
                     (N2 // 2) * t + c2 - RING2 // 2 + 1)
                buf = step_buf((N2 * s + HF * c2 + h) % RING2)
                pair_ = cv[:, 2 * (c2 % 2):2 * (c2 % 2) + 2, 0:CW]
                v.wait_ge(bn_ready, 1)
                v.scalar_tensor_tensor(buf.rearrange("p (e c) -> p e c", e=2),
                                       chunk(s, h, 2 * c2, 2).rearrange("p (e c) -> p e c", e=2),
                                       gmA[:, n, h:h + 1], pair_, ALU.subtract, ALU.mult).then_inc(prod_done, 1)

            def add(t, s, c2):
                k = N2 * t + HF * c2
                v.wait_ge(act_done, k + 1)
                at = chunk(s, 0, 2 * c2, 2)
                v.tensor_tensor(at, at, step_buf((N2 * s + HF * c2) % RING2), ALU.add).then_inc(add_dve, 1)

            def phase2(t, s, n, back):
                if back is not None:
                    v.wait_ge(x1_back[s], back)
                v.tensor_copy(bAs[:, s, :], bA[:, n, :])
                for c2 in range(CH // 2):
                    product(t, s, c2, 0, n)
                    product(t, s, c2, 1, n)
                    if c2 > 0:
                        add(t, s, c2 - 1)
                add(t, s, CH // 2 - 1)

            for s in range(SLOTS):
                phase2(s, s, NB - SLOTS + s, None)
            with v.Fori(1, NB // SLOTS) as q:
                for s in range(SLOTS):
                    phase2(SLOTS * q + s, s, SLOTS * (q - 1) + s, 16 * q)


def kernel(**inputs):
    import numpy as np
    import concourse.bacc as bacc
    from concourse.bass_utils import run_bass_kernel_spmd

    x = np.asarray(inputs["x"])
    n = x.shape[0]
    halves = lambda a: np.ascontiguousarray(np.asarray(a).reshape(2, P).T)
    by_state = lambda a: np.repeat(np.asarray(a).reshape(-1), CH)
    every = lambda a: np.repeat(np.asarray(a).reshape(-1), P)
    w1 = np.asarray(inputs["L1_conv_ca_w1"])
    arrays = {
        "x": np.ascontiguousarray(x.reshape(n, PX, 2, P).transpose(0, 2, 3, 1)),
        "w": np.ascontiguousarray(np.asarray(inputs["L0_conv_W"]).reshape(TAPS * 2, P, 2 * P)),
        "bias": halves(inputs["L0_conv_b"]),
        "w1": np.ascontiguousarray(w1.T.reshape(2, P, RED).transpose(1, 0, 2)),
        "w2": np.ascontiguousarray(np.asarray(inputs["L1_conv_ca_w2"]).T),
        "lsa": np.ascontiguousarray(np.asarray(inputs["L1_conv_lsa_w"]).reshape(-1)),
        "scal": np.ascontiguousarray(np.stack(
            [by_state(inputs["L1_conv_A"]), by_state(inputs["L1_conv_B_w"]), by_state(inputs["L1_conv_B_b"]),
             by_state(inputs["L1_conv_C_w"]), by_state(inputs["L1_conv_C_b"]),
             every(inputs["L1_conv_d_w"]), every(inputs["L1_conv_d_b"])], axis=1)),
        "bn": np.ascontiguousarray(np.stack([halves(inputs["L1_conv_bn_gamma"]), halves(inputs["L1_conv_bn_beta"])], axis=1)),
    }
    nc = bacc.Bacc("TRN2", target_bir_lowering=False, num_devices=1)
    args = [nc.dram_tensor(f"in_{k}", a.shape, F32, kind="ExternalInput").ap() for k, a in arrays.items()]
    out = nc.dram_tensor("out", (n, 2, P, PX), F32, kind="ExternalOutput").ap()
    by_name = dict(zip(arrays, args))
    build_kernel(nc, by_name["x"], by_name["w"], by_name["bias"], by_name["w1"], by_name["w2"], by_name["lsa"],
                 by_name["scal"], by_name["bn"], out)
    r = run_bass_kernel_spmd(nc, [{f"in_{k}": a for k, a in arrays.items()}], core_ids=[0])
    got = r.results[0]["out"]
    return np.ascontiguousarray(got.reshape(n, 2, P, PX).transpose(0, 3, 1, 2).reshape(n, H, W, 2 * P))
```

```python
from contextlib import ExitStack

import concourse.bass as bass
from concourse import mybir

F32 = mybir.dt.float32
F16 = mybir.dt.float16
I32 = mybir.dt.int32
ALU = mybir.AluOpType
ACT = mybir.ActivationFunctionType
AX_X = mybir.AxisListType.X

P = 128
HF = 2
H = W = 56
PX = H * W
CH = 8
R = H // CH
CW = R * W
UN = CH * HF
SQ = 32
GC = 7
GW = PX // GC
GB = GW // SQ
NQ = PX // SQ
TAPS = 9
ST = 16
RED = 16
GS = 8
K7 = 7
PAD7 = K7 // 2
BAND = 2 * H - 1
MAXROW = 64
SLOTS = 4
ROWS = 3
RING = 6
CLAMP = -80.0

PREP = {9: [0], 10: [1, 2], 11: [3], 12: [4], 14: [5]}
PREP_OWN = [6, 7]
WSTAT = {9: [0], 10: [1], 11: [2], 12: [3], 13: [4], 14: [5], 15: [6, 7]}
GATE0 = 7

SPREAD = [0, 4, 1, 5, 2, 6, 3, 7]
HELP = [4, 5, 6, 7]
OWN = [c for c in SPREAD if c not in HELP]
BEFORE_B = [0, 1, 2, 3]
WITHIN_B = {0: [4], 3: [5], 5: [6], 6: [7]}
DEVIATIONS = {0: [4, 5], 3: [6, 7]}
STEPS = 8


class Live:

    def __init__(self, i, n_images):
        self.conv = 0 <= i < n_images
        self.next = 0 <= i + 1 < n_images
        self.a = 0 <= i - 1 < n_images
        self.b = 0 <= i - 2 < n_images


def iterations(eng, n_images, work):
    full = Live(2, 4)
    for i in range(-1, 2):
        work(i, Live(i, n_images))
    with eng.Fori(2, n_images - 1) as i:
        work(i, full)
    work(n_images - 1, Live(n_images - 1, n_images))


def steps(eng, n_images, step):
    rounds = n_images // RING
    for s in range(RING):
        step(0, s)
    if rounds > 1:
        with eng.Fori(1, rounds) as q:
            for s in range(RING):
                step(q, s)
    for s in range(n_images % RING):
        step(rounds, s)


def wait(eng, sem, value):
    if not isinstance(value, int) or value > 0:
        eng.wait_ge(sem, value)


def build_kernel(nc, x, w, bias, w1, w2, lsa, scal, bn, out):
    NB = x.shape[0]
    assert NB >= RING + 1
    WCOLS = TAPS * HF * 2 * P

    ctx = ExitStack()
    with ctx:
        def sb(name, shape, dt=F32):
            return ctx.enter_context(nc.sbuf_tensor(name, shape, dt))

        def bank(name, n=1):
            return ctx.enter_context(nc.psum_tensor(name, [P, n, 512], F32))

        def sem(name):
            return ctx.enter_context(nc.semaphore(name))

        x1_dram = nc.dram_tensor("x1_dram", (NB, HF, P, PX), F32, kind="Internal").ap()
        feat_dram = nc.dram_tensor("feat_dram", (2, PX), F32, kind="Internal").ap()
        g_dram = nc.dram_tensor("g_dram", (NB, PX), F32, kind="Internal").ap()
        band_dram = nc.dram_tensor("band_dram", (P, K7, BAND), F32, kind="Internal").ap()

        xs = sb("xs", [P, SLOTS, HF, PX])
        hl = sb("hl", [P, 2, HF, PX], F16)
        spare = [sb("spare0", [P, WCOLS // 2 + 4 * CW]), sb("spare1", [P, 4 * CW + 4 * GW])]
        tern = spare[0][:, 0:WCOLS // 2].bitcast(F16).rearrange(
            "p (t k m) -> p t k m", t=TAPS, k=HF)
        xn = sb("xn", [P, 2, HF, CW])
        rl = spare[0][:, WCOLS // 2:].rearrange("p (u c) -> p u c", c=CW)
        xc = sb("xc", [P, 2, HF, GW])
        xp, xt = (spare[1][:, 4 * CW + k * 2 * GW:4 * CW + (k + 1) * 2 * GW].rearrange("p (a c) -> p a c", a=2)
                  for k in range(2))
        wk = spare[1][:, 0:4 * CW].rearrange("p (b h c) -> p b h c", b=2, h=HF)
        gB = sb("gB", [P, PX])

        ident = sb("ident", [P, P])
        ones = sb("ones", [P, P])
        gmat = sb("gmat", [P, P])
        selr = sb("selr", [P, R, H])
        lw = sb("lw", [P, K7, K7, 2])
        band = gB[:, 0:K7 * BAND].rearrange("p (a b) -> p a b", b=BAND)
        toep = sb("toep", [P, K7, H])
        rmask = sb("rmask", [1, P])
        pidx = sb("pidx", [P, 1], I32)
        pj = sb("pj", [P, 1], I32)
        pjf = sb("pjf", [P, 1])
        tgt = sb("tgt", [P, R])
        iot = sb("iot", [P, H])

        w1T = sb("w1T", [P, HF, RED])
        w2T = sb("w2T", [RED, HF * P])
        biasc = sb("biasc", [P, HF])
        sv = sb("sv", [P, 7])
        bnp = sb("bnp", [P, 2, HF])
        wstat = sb("wstat", [P, 8])
        alpha = sb("alpha", [P, 1])
        tick = sb("tick", [1, 1])

        st = [sb(f"st{q}", [P, HF, CH, 6]) for q in range(2)]
        stw = sb("stw", [P, HF, CH, 6])
        mv = [sb(f"mv{q}", [P, HF, 2]) for q in range(2)]
        gm = [sb(f"gm{q}", [P, HF]) for q in range(2)]
        dq = [sb(f"dq{q}", [P, HF]) for q in range(2)]
        dv = [sb(f"dv{q}", [P, HF]) for q in range(2)]
        vv = [sb(f"vv{q}", [P, HF]) for q in range(3)]
        lnv = [sb(f"lnv{q}", [P, HF]) for q in range(3)]
        r0 = [sb(f"r0{q}", [P, HF]) for q in range(3)]
        nt = [sb(f"nt{q}", [P, HF]) for q in range(3)]
        rs = [sb(f"rs{q}", [P, HF]) for q in range(3)]
        mx1 = sb("mx1", [P, CH, HF])
        fmx = sb("fmx", [P, HF])
        fd = sb("fd", [P, HF, 2])
        fv = sb("fv", [P, HF, 2])
        hr = sb("hr", [RED, 2])
        hs = sb("hs", [RED, 1])
        garg = sb("garg", [P, HF])
        gexp = sb("gexp", [P, HF])
        gden = sb("gden", [P, HF])
        gate = sb("gate", [P, HF])
        kcur = sb("kcur", [P, HF])
        nb = sb("nb", [P, HF])
        nbx = sb("nbx", [P, HF])
        ngm = sb("ngm", [P, 2, HF])
        red = sb("red", [P, 2, NQ])
        maps = sb("maps", [NQ, 2, SQ])
        feat = sb("feat", [P, W + 2 * PAD7])

        ms = sb("ms", [P, CW])
        zs = sb("zs", [P, CW])
        nz = sb("nz", [P, CW])
        es = sb("es", [P, CW])
        us = sb("us", [P, CW])
        ls = sb("ls", [P, CW])
        de = sb("de", [P, CW])
        dA = sb("dA", [P, CW])
        sumd = sb("sumd", [P, 1])
        pend = sb("pend", [P, 1])
        rp = sb("rp", [1, P])
        rh = sb("rh", [1, P])
        rH = sb("rH", [1, P])
        hin = sb("hin", [1, P])
        hinc = sb("hinc", [P, 1])
        sy = sb("sy", [H, 2, W])
        sye = sb("sye", [H, 2, W])
        syd = sb("syd", [H, 2, W])
        syr = sb("syr", [H, 2, W])
        g56 = sb("g56", [H, W])
        mwt = sb("mwt", [P, HF, 2])

        gmA = sb("gmA", [P, NB, HF])
        kA = sb("kA", [P, NB, HF])
        mwA = sb("mwA", [P, NB, HF, 2])
        bm = sb("bm", [P, NB, HF])
        bq = sb("bq", [P, NB, HF])
        bs = sb("bs", [P, HF])
        bmean = sb("bmean", [P, HF])
        bscale = sb("bscale", [P, HF])
        bA = sb("bA", [P, NB, HF])
        bAs = sb("bAs", [P, RING, HF])
        bB = sb("bB", [P, HF])

        cv = bank("cv", 4)
        Mb = bank("Mb")
        TR = bank("TR")
        SA = bank("SA")
        SB = bank("SB")
        S7 = Mb[0:H, 0, 0:W]
        TRv = TR[0:NQ, 0, 0:2 * P].rearrange("p (a q i) -> p a i q", a=2, i=SQ)
        ROWP = SB[0:1, 0, 128:256]
        ROWH = SB[0:1, 0, 256:384]
        HIN = SB[:, 0, 384:385]
        Y56 = SB[0:H, 0, 400:400 + W]

        params = sem("params"); w_loaded = sem("w_loaded"); lw_loaded = sem("lw_loaded")
        pool_const = sem("pool_const"); pool_zero = sem("pool_zero"); wa_ready = sem("wa_ready"); dve_const = sem("dve_const")
        w_tot = sem("w_tot"); w_cnt = sem("w_cnt"); w_cnt_tot = sem("w_cnt_tot")
        w_ready = sem("w_ready"); tern_ready = sem("tern_ready"); band_ready = sem("band_ready"); band_stored = sem("band_stored")
        toep_ready = sem("toep_ready")
        x_loaded = sem("x_loaded"); x1_stored = sem("x1_stored")
        norm_ready = sem("norm_ready"); hi_done = sem("hi_done"); lo_done = sem("lo_done")
        conv_done = sem("conv_done"); relu_done = sem("relu_done"); x1_done = sem("x1_done")
        mean_in = [sem(f"mean_in{q}") for q in range(2)]
        mean_out = [sem(f"mean_out{q}") for q in range(2)]
        var_in = [sem(f"var_in{q}") for q in range(2)]
        var_out = [sem(f"var_out{q}") for q in range(2)]
        v_ready = [sem(f"v_ready{q}") for q in range(3)]
        rs_guess = [sem(f"rs_guess{q}") for q in range(3)]
        fc1_in = sem("fc1_in"); fc1_out = sem("fc1_out"); fc2_in = sem("fc2_in"); fc2_out = sem("fc2_out")
        gate_arg = sem("gate_arg"); gate_exp = sem("gate_exp"); gate_done = sem("gate_done")
        xc_done = sem("xc_done"); pair_sum_done = sem("pair_sum_done"); pair_max_done = sem("pair_max_done"); turned = sem("turned")
        red_ready = sem("red_ready"); red_turned = sem("red_turned"); maps_ready = sem("maps_ready")
        maps_stored = sem("maps_stored"); ms_loaded = sem("ms_loaded"); ms_read = sem("ms_read")
        nz_ready = sem("nz_ready"); e_ready = sem("e_ready"); u_ready = sem("u_ready"); l_ready = sem("l_ready")
        delta_ready = sem("delta_ready"); decay_ready = sem("decay_ready"); ends_ready = sem("ends_ready")
        rows_out = sem("rows_out"); hin_ready = sem("hin_ready"); hin_out = sem("hin_out")
        hc_ready = sem("hc_ready"); y_done = sem("y_done"); c7_done = sem("c7_done"); s_taken = sem("s_taken")
        sy_ready = sem("sy_ready"); sye_ready = sem("sye_ready"); g_ready = sem("g_ready")
        feat_loaded = sem("feat_loaded")
        g_stored = sem("g_stored"); g_spread = sem("g_spread"); w_done = sem("w_done")
        row_ready = sem("row_ready"); row_done = sem("row_done"); row_stored = sem("row_stored"); row_loaded = sem("row_loaded")
        dev_ready = sem("dev_ready"); ngm_ready = sem("ngm_ready")
        w_made = sem("w_made"); g_rows = sem("g_rows"); g_used = sem("g_used"); g_copied = sem("g_copied")
        bn_ready = sem("bn_ready"); grow_loaded = [sem(f"grow_loaded{k}") for k in range(ROWS)]
        x1_back = [sem(f"x1_back{k}") for k in range(RING)]
        out_stored = [sem(f"out_stored{k}") for k in range(RING)]
        spread = sem("spread"); prod_done = sem("prod_done"); act_done = sem("act_done")
        add_dve = sem("add_dve"); add_pool = sem("add_pool")

        C2 = 2 * CW
        N2 = CH // 2 * HF
        RING2 = 4
        ring2 = [xn[:, :, :, :].rearrange("p a h c -> p (a h c)"), xc[:, :, :, :].rearrange("p a h c -> p (a h c)")]
        hl32 = hl[:, :, :, :].rearrange("p a h x -> p (a h x)").bitcast(F32)
        PIECES = [1] * (RING - 1) + [HF]
        growt = gB

        row = hl32[0:1, 0:PX]
        w_ring = [wk[:, 0], wk[:, 1], xn[:, 0], xn[:, 1]]
        w_help = [xn[:, 0], xn[:, 1], xc[:, 0, :, 0:CW], xc[:, 1, :, 0:CW]]
        LAST = NB - 1

        wj, wv, wa = (xs[:, k, :, :].rearrange("p h x -> p (h x)")[:, 0:WCOLS] for k in (1, 2, 3))

        def chunk(slot, h, c, n=1):
            return xs[:, slot, h, c * CW:(c + n) * CW]

        def rows(ap):
            return ap.rearrange("p (r w) -> p r w", w=W)

        def pixels(s, h, c2):
            a = xs[:, s, h, :] if s < SLOTS else hl32[:, h * PX:(h + 1) * PX] if s == SLOTS else spare[h]
            return a[:, c2 * C2:(c2 + 1) * C2]

        def moves(s, dram, cols=slice(0, PX)):
            if s < SLOTS:
                return [(xs[:, s, :, cols], dram[:, :, cols].rearrange("h p x -> p h x"))]
            if s == SLOTS:
                whole = hl32[:, 0:HF * PX].rearrange("p (h x) -> p h x", h=HF)
                return [(whole[:, :, cols], dram[:, :, cols].rearrange("h p x -> p h x"))]
            return [(spare[h][:, cols], dram[h, :, cols]) for h in range(HF)]

        def image_of(q, s):
            return NB - SLOTS + s if isinstance(q, int) and q == 0 and s < SLOTS else RING * q + s - SLOTS

        def by_pool(c2, h):
            return h == 1 or c2 == 0

        def added(t, c2, h):
            order = [(c, e) for c in range(CH // 2) for e in range(HF)]
            mine = [(c, e) for c, e in order if by_pool(c, e) == by_pool(c2, h)]
            return add_pool if by_pool(c2, h) else add_dve, t * len(mine) + (mine.index((c2, h)) + 1)

        def step_buf(k):
            return ring2[k // 2][:, (k % 2) * C2:(k % 2) * C2 + C2]

        block = ctx.enter_context(nc.Block())

        @block.sync
        def _(sp):
            sp.dma_start(xs[:, 0, :, :], x[0].rearrange("h p x -> p h x")).then_inc(x_loaded, 16)
            sp.dma_start(wv.rearrange("p (t m) -> p t m", m=2 * P),
                         w.rearrange("t p m -> p t m")).then_inc(w_loaded, 16)
            sp.dma_start(biasc[:, :], bias).then_inc(params, 16)
            sp.dma_start(w1T[:, :, :], w1).then_inc(params, 16)
            sp.dma_start(w2T[:, :], w2).then_inc(params, 16)
            sp.dma_start(sv[:, :], scal).then_inc(params, 16)
            sp.dma_start(bnp[:, :, :], bn).then_inc(params, 16)
            sp.dma_start(lw[:, :, :, :].rearrange("p a b c -> p (a b c)"), lsa.partition_broadcast(P)).then_inc(lw_loaded, 16)
            sp.wait_ge(band_ready, 1)
            sp.dma_start(band_dram, band).then_inc(band_stored, 16)
            sp.wait_ge(band_stored, 16)
            for c in range(2):
                src = bass.AP(tensor=band_dram.tensor, offset=c * MAXROW * K7 * BAND + H - 1,
                              ap=[[K7 * BAND - 1, H], [BAND, K7], [1, H]])
                sp.dma_start(toep[c * MAXROW:c * MAXROW + H, :, :], src).then_inc(toep_ready, 16)

            def gate_map(n):
                sp.wait_ge(g_ready, n + 1)
                sp.dma_start(g_dram[n].rearrange("(a b) -> a b", b=W), g56[:, :]).then_inc(g_stored, 16)

            def spread_gate(n):
                sp.wait_ge(g_stored, 16 * (n + 1))
                sp.dma_start(gB[:, :], g_dram[n].partition_broadcast(P)).then_inc(g_spread, 16)

            def load_maps():
                sp.dma_start(ms[:, :], bass.AP(tensor=feat_dram.tensor, offset=0,
                                               ap=[[0, ST], [CW, CH], [1, CW]])).then_inc(ms_loaded, 16)
                for c in range(2):
                    sp.dma_start(feat[c * MAXROW:c * MAXROW + H, PAD7:PAD7 + W],
                                 feat_dram[c].rearrange("(a b) -> a b", b=W)).then_inc(feat_loaded, 16)

            def work(i, live):
                if live.next and not (isinstance(i, int) and i < 0):
                    n = i + 1
                    if not isinstance(i, int) or i >= 2:
                        sp.wait_ge(x1_stored, 16 * (i - 1))
                        sp.wait_ge(ms_read, i - 1)
                    elif i == 0:
                        sp.wait_ge(w_ready, 1)
                    sp.wait_ge(x_loaded, 16 * n)
                    sp.dma_start(xs[:, n % SLOTS, :, :], x[n].rearrange("h p x -> p h x")).then_inc(x_loaded, 16)
                if live.a and not (isinstance(i, int) and i == LAST):
                    sp.wait_ge(x1_done, UN * i)
                    wait(sp, x1_stored, 16 * (i - 1))
                    sp.dma_start(x1_dram[i - 1].rearrange("h p x -> p h x"),
                                 xs[:, (i - 1) % SLOTS, :, :]).then_inc(x1_stored, 16)
                if live.b:
                    gate_map(i - 2)
                    spread_gate(i - 2)
                if live.a:
                    n = i - 1
                    sp.wait_ge(maps_ready, n + 1)
                    sp.dma_start(feat_dram.rearrange("c (b x) -> b c x", x=SQ), maps[:, :, :]).then_inc(maps_stored, 16)
                    if live.b:
                        sp.wait_ge(hc_ready, i - 1)
                        sp.wait_ge(c7_done, i - 1)
                    sp.wait_ge(maps_stored, 16 * (n + 1))
                    load_maps()

            iterations(sp, NB, work)

            gate_map(LAST - 1)
            spread_gate(LAST - 1)
            sp.wait_ge(x1_stored, 16 * (NB - 2))
            sp.wait_ge(x1_done, UN * NB)
            back = moves(RING - 1, x1_dram[1])
            sp.dma_start(*back[0]).then_inc(x1_back[RING - 1], 16)
            sp.wait_ge(row_done, GC)
            sp.dma_start(feat_dram[0:1], row).then_inc(row_stored, 16)
            sp.wait_ge(maps_ready, NB)
            sp.dma_start(feat_dram[1].rearrange("(b x) -> b x", x=SQ), maps[:, 1, :]).then_inc(maps_stored, 16)
            sp.wait_ge(hc_ready, LAST)
            sp.wait_ge(c7_done, LAST)
            sp.wait_ge(row_stored, 16)
            sp.wait_ge(maps_stored, 16 * NB)
            load_maps()
            gate_map(LAST)
            sp.wait_ge(g_stored, 16 * NB)
            sp.dma_start(row, g_dram[LAST].rearrange("(a b) -> a b", a=1)).then_inc(row_loaded, 16)

            sp.wait_ge(g_rows, CH)
            halves = [moves(SLOTS, x1_dram[0], slice(k * PX // 2, (k + 1) * PX // 2))[0] for k in range(2)]
            sp.dma_start(*halves[0]).then_inc(x1_back[SLOTS], 16)
            sp.wait_ge(w_done, CH * NB)

            def grow(t):
                k = t % ROWS
                sp.dma_start(growt[32 * k:32 * k + 1, :],
                             g_dram[image_of(t // RING, t % RING)].rearrange("(a b) -> a b", a=1)).then_inc(grow_loaded[k], 16)

            def stored(s, images):
                return 16 * PIECES[s] * (2 * images + (2 if s == 0 else 0))

            def refill(t):
                q, s = divmod(t, RING)
                if t + RING < NB:
                    sp.wait_ge(out_stored[s], stored(s, q + 1))
                    for onchip, dram in moves(s, x1_dram[image_of(q + 1, s)]):
                        sp.dma_start(onchip, dram).then_inc(x1_back[s], 16)

            for t in range(ROWS):
                grow(t)
            sp.dma_start(*halves[1]).then_inc(x1_back[SLOTS], 16)
            sp.dma_start(*back[1]).then_inc(x1_back[RING - 1], 16)
            for t in range(NB):
                s = t % RING
                parts = 4 if t == 0 else 2
                for part in range(parts):
                    for h in range(HF):
                        sp.wait_ge(*added(t, (part + 1) * CH // 2 // parts - 1, h))
                    cols = slice(part * PX // parts, (part + 1) * PX // parts)
                    for onchip, dram in moves(s, out[image_of(t // RING, s)], cols):
                        sp.dma_start(dram, onchip).then_inc(out_stored[s], 16)
                    if part == 0 and t > 1:
                        refill(t - 1)
                if t == 0:
                    refill(0)
                if t + ROWS < NB:
                    grow(t + ROWS)
            for s in range(RING):
                sp.wait_ge(out_stored[s], stored(s, len(range(s, NB, RING))))

        @block.gpsimd
        def _(pool):
            pool.memset(ident[:, :], 0.0).then_inc(pool_const, 1)
            pool.memset(gmat[:, :], 1.0 / GS).then_inc(pool_const, 1)
            pool.memset(ones[:, :], 1.0).then_inc(pool_const, 1)
            pool.memset(band, 0.0).then_inc(pool_zero, 1)
            pool.memset(feat[:, :], 0.0).then_inc(pool_zero, 1)
            pool.memset(toep[:, :, :], 0.0).then_inc(pool_zero, 1)
            pool.memset(hin[:, :], 0.0).then_inc(pool_zero, 1)
            pool.iota(pidx[:, :], pattern=[[0, 1]], base=0, channel_multiplier=1).then_inc(pool_const, 1)
            pool.iota(iot[:, :], pattern=[[1, H]], base=0, channel_multiplier=0,
                      allow_small_or_imprecise_dtypes=True).then_inc(pool_const, 1)
            pool.wait_ge(pool_const, 5)
            pool.affine_select(out=ident[:, :], in_=ident[:, :], compare_op=ALU.not_equal, fill=1.0, base=0,
                               pattern=[[-1, P]], channel_multiplier=1).then_inc(pool_const, 1)
            g3 = gmat[:, :].rearrange("p (a b) -> p a b", b=GS)
            pool.affine_select(out=g3, in_=g3, compare_op=ALU.is_ge, fill=0.0, base=0,
                               pattern=[[-GS, P // GS], [0, GS]], channel_multiplier=1).then_inc(pool_const, 1)
            pool.wait_ge(pool_const, 7)
            pool.affine_select(out=g3, in_=g3, compare_op=ALU.is_ge, fill=0.0, base=GS - 1,
                               pattern=[[GS, P // GS], [0, GS]], channel_multiplier=-1).then_inc(pool_const, 1)

            def residual(n, u):
                b, o = divmod(u, HF)
                pool.wait_ge(relu_done, UN * n + u + 1)
                pool.wait_ge(w_ready, 1)
                at = chunk(n % SLOTS, o, b)
                pool.tensor_tensor(at, at, rl[:, u % 4, :], ALU.add).then_inc(x1_done, 1)

            def low(n, c):
                pool.wait_ge(hi_done, CH * n + c + 1)
                at = slice(c * CW, (c + 1) * CW)
                pool.tensor_tensor(hl[:, 1, :, at], xn[:, c % 2, :, :], hl[:, 0, :, at], ALU.subtract).then_inc(lo_done, 1)

            def pair_sum(n, c):
                pool.wait_ge(xc_done, GC * n + c + 1)
                wait(pool, turned, GC * n + c)
                pool.tensor_tensor(xp[:, 0, :], xc[:, c % 2, 0, :], xc[:, c % 2, 1, :], ALU.add).then_inc(pair_sum_done, 1)

            def work(i, live):
                for u in range(UN):
                    if u == 0 and live.conv:
                        for c in PREP_OWN:
                            if c == PREP_OWN[0] and live.a:
                                residual(i - 1, UN - 1)
                            low(i, c)
                    elif u == 0 and live.a:
                        residual(i - 1, UN - 1)
                    if u > 0 and live.conv:
                        residual(i, u - 1)
                    if live.a and GATE0 <= u < GATE0 + GC:
                        pair_sum(i - 1, u - GATE0)
                    if live.next:
                        for c in PREP.get(u, []):
                            low(i + 1, c)

            iterations(pool, NB, work)

            residual(LAST, UN - 1)
            pool.drain()

            def deviation(n, c, buf):
                for h in range(HF):
                    pool.tensor_scalar(buf[:, h, :], chunk(n % SLOTS, h, c), gmA[:, n, h:h + 1], None, ALU.subtract)

            def times_gate(c, buf):
                for h in range(HF):
                    last = pool.tensor_tensor(buf[:, h, :], buf[:, h, :], gB[:, c * CW:(c + 1) * CW], ALU.mult)
                last.then_inc(w_made, 1)

            pool.wait_ge(w_done, CH * (LAST - 1))
            for c in range(len(w_ring)):
                deviation(LAST - 1, c, w_ring[c])
            pool.drain()
            pool.wait_ge(g_spread, 16 * LAST)
            for c in range(CH):
                if c >= len(w_ring):
                    pool.wait_ge(dev_ready, c - len(w_ring) + 1)
                times_gate(c, w_ring[c % len(w_ring)])
            for k, c in enumerate(HELP):
                pool.wait_ge(dev_ready, CH - len(w_ring) + k + 1)
                pool.wait_ge(g_copied, k + 1)
                times_gate(c, w_help[k])

            def phase2(q, s):
                for c2 in range(CH // 2):
                    for h in range(HF):
                        if by_pool(c2, h):
                            pool.wait_ge(act_done, N2 * (RING * q + s) + HF * c2 + h + 1)
                            at = pixels(s, h, c2)
                            pool.tensor_tensor(at, at, step_buf((N2 * s + HF * c2 + h) % RING2), ALU.add).then_inc(add_pool, 1)

            steps(pool, NB, phase2)

        @block.scalar
        def _(act):
            def relu(n, u):
                b, o = divmod(u, HF)
                act.wait_ge(conv_done, UN * n + u + 1)
                wait(act, x1_done, UN * n + u - 3)
                act.wait_ge(w_ready, 1)
                act.activation(rl[:, u % 4, :], cv[:, u % 4, 0:CW], ACT.Relu, bias=biasc[:, o:o + 1],
                               scale=alpha[:, 0:1]).then_inc(relu_done, 1)

            def high(n, c):
                act.wait_ge(norm_ready, n + 1)
                wait(act, lo_done, CH * n + c - 1)
                act.wait_ge(pool_zero, 4)
                for h in range(HF):
                    act.activation(xn[:, c % 2, h, :], chunk(n % SLOTS, h, c), ACT.Identity,
                                   bias=nbx[:, h:h + 1], scale=rs[0][:, h:h + 1])
                act.drain()
                wait(act, conv_done, UN * (n - 1) + 2 * min(c + 1, CH - 1) + 2)
                act.wait_ge(pool_zero, 4)
                act.copy(hl[:, 0, :, c * CW:(c + 1) * CW], xn[:, c % 2, :, :]).then_inc(hi_done, 1)

            def rsqrt_guess(q, count):
                act.wait_ge(v_ready[q], count)
                act.activation(lnv[q][:, :], vv[q][:, :], ACT.Ln)
                act.drain()
                act.activation(r0[q][:, :], lnv[q][:, :], ACT.Exp, scale=-0.5).then_inc(rs_guess[q], 1)

            def gated(n, c):
                act.wait_ge(gate_done, n + 1)
                wait(act, pair_sum_done, GC * n + c - 1)
                wait(act, pair_max_done, GC * n + c - 1)
                act.wait_ge(w_ready, 1)
                for h in range(HF):
                    last = act.activation(xc[:, c % 2, h, :], xs[:, n % SLOTS, h, c * GW:(c + 1) * GW], ACT.Identity,
                                          bias=nb[:, h:h + 1], scale=kcur[:, h:h + 1])
                last.then_inc(xc_done, 1)

            def stage_b(n, u):
                if u == 0:
                    act.wait_ge(nz_ready, n + 1)
                    act.activation(es[:, :], nz[:, :], ACT.Exp).then_inc(e_ready, 1)
                if u == 1:
                    act.wait_ge(u_ready, n + 1)
                    act.activation(ls[:, :], us[:, :], ACT.Ln).then_inc(l_ready, 1)
                if u == 2:
                    act.wait_ge(delta_ready, n + 1)
                    act.activation(dA[:, :], de[:, :], ACT.Exp, scale=sv[:, 0:1])
                    act.activation(pend[:, :], sumd[:, :], ACT.Exp, scale=sv[:, 0:1]).then_inc(decay_ready, 1)
                if u == 6:
                    act.wait_ge(sy_ready, n + 1)
                    act.activation(sye[:, :, :], sy[:, :, :], ACT.Exp, scale=-1.0).then_inc(sye_ready, 1)

            def stage_a(n, u):
                if u == 3:
                    rsqrt_guess(1, n + 1)
                if u == 6:
                    act.wait_ge(gate_arg, n + 1)
                    act.activation(gexp[:, :], garg[:, :], ACT.Exp, scale=-1.0).then_inc(gate_exp, 1)

            def work(i, live):
                for u in range(UN):
                    if u == 0 and live.conv:
                        for c in PREP_OWN:
                            if c == PREP_OWN[0] and live.a:
                                relu(i - 1, UN - 1)
                            high(i, c)
                    elif u == 0 and live.a:
                        relu(i - 1, UN - 1)
                    if u > 0 and live.conv:
                        relu(i, u - 1)
                    if live.b:
                        stage_b(i - 2, u)
                    if live.a:
                        stage_a(i - 1, u)
                    if live.next and u == 8:
                        rsqrt_guess(0, i + 2)
                    if live.a and GATE0 <= u < GATE0 + GC:
                        gated(i - 1, u - GATE0)
                    if live.next:
                        for c in PREP.get(u, []):
                            high(i + 1, c)

            act.wait_ge(w_loaded, 16)
            act.activation(wa, wv, ACT.Abs, accum_out=wstat[:, 0:1]).then_inc(wa_ready, 1)
            act.wait_ge(params, 5 * 16)
            iterations(act, NB, work)

            relu(LAST, UN - 1)
            for u in range(STEPS):
                stage_b(LAST - 1, u)
                stage_a(LAST, u)

            def copy_row(c):
                act.wait_ge(row_ready, c + 1)
                act.activation(row[:, c * GW:(c + 1) * GW], cv[0:1, c % 2, 0:GW], ACT.Copy,
                               scale=1.0 / (HF * P)).then_inc(row_done, 1)

            act.wait_ge(gate_done, NB)
            for c in range(GC):
                if c >= 2:
                    act.wait_ge(row_ready, c - 1)
                    act.wait_ge(pair_max_done, GC * LAST + c - 1)
                for h in range(HF):
                    last = act.activation(xc[:, c % 2, h, :], xs[:, LAST % SLOTS, h, c * GW:(c + 1) * GW], ACT.Identity,
                                          bias=nb[:, h:h + 1], scale=kcur[:, h:h + 1])
                last.then_inc(xc_done, 1)
                if c > 0:
                    copy_row(c - 1)
            copy_row(GC - 1)

            def deviation(n, c, buf):
                for h in range(HF):
                    last = act.activation(buf[:, h, :], chunk(n % SLOTS, h, c), ACT.Identity, bias=ngm[:, LAST - n, h:h + 1])
                last.then_inc(dev_ready, 1)

            act.wait_ge(ngm_ready, 1)
            for u in range(STEPS):
                for c in DEVIATIONS.get(u, []):
                    act.wait_ge(w_done, CH * (LAST - 1) + c - len(w_ring) + 1)
                    deviation(LAST - 1, c, w_ring[c % len(w_ring)])
                stage_b(LAST, u)
            act.wait_ge(w_done, CH * LAST)
            for k, c in enumerate(HELP):
                deviation(LAST, c, w_help[k])
            for k, c in enumerate(HELP):
                j = SPREAD.index(c)
                act.wait_ge(g_rows, j + 1)
                act.copy(gB[:, c * CW:(c + 1) * CW], cv[:, j % 4, 0:CW]).then_inc(g_copied, 1)
            rsqrt_guess(2, 1)

            def phase2(q, s):
                for c2 in range(CH // 2):
                    for h in range(HF):
                        k = N2 * (RING * q + s) + HF * c2 + h
                        act.wait_ge(prod_done, k + 1)
                        act.wait_ge(bn_ready, 1)
                        buf = step_buf((N2 * s + HF * c2 + h) % RING2)
                        act.activation(buf, buf, ACT.Relu, bias=bB[:, h:h + 1],
                                       scale=bAs[:, s, h:h + 1]).then_inc(act_done, 1)

            steps(act, NB, phase2)

        @block.tensor
        def _(pe):
            def conv(n, u):
                b, o = divmod(u, HF)
                wait(pe, relu_done, UN * n + u - 3)
                if u == 0:
                    pe.wait_ge(lo_done, CH * n + 1)
                order = [(k, dy, dx, part) for dy in (1, 0, 2) for dx in (1, 0, 2) for k in range(HF) for part in range(2)]
                to = rows(cv[:, u % 4, 0:CW])
                for at, (k, dy, dx, part) in enumerate(order):
                    if o == 0 and b < CH - 1 and at == order.index((0, 2, 1, 0)):
                        pe.wait_ge(lo_done, CH * n + b + 2)
                    ra, rb = (1 if b == 0 and dy == 0 else 0), (R - 1 if b == CH - 1 and dy == 2 else R)
                    ca, cb = (1 if dx == 0 else 0), (W - 1 if dx == 2 else W)
                    last = pe.matmul(to[:, ra:rb, ca:cb], tern[:, 3 * dy + dx, k, o * P:(o + 1) * P],
                                     rows(hl[:, part, k, :])[:, R * b + dy - 1 + ra:R * b + dy - 1 + rb, dx - 1 + ca:dx - 1 + cb],
                                     start=(at == 0), stop=(at == len(order) - 1))
                last.then_inc(conv_done, 1)

            def group_mean(q, count):
                pe.wait_ge(mean_in[q], count)
                pe.matmul(SA[:, 0, 4 * q:4 * q + 2], gmat[:, :], mv[q][:, :, 0], start=True, stop=True).then_inc(mean_out[q], 1)

            def group_var(q, count):
                pe.wait_ge(var_in[q], count)
                pe.matmul(SA[:, 0, 4 * q + 2:4 * q + 4], gmat[:, :], dv[q][:, :], start=True, stop=True).then_inc(var_out[q], 1)

            def stage_b(n, u):
                if u == 3:
                    pe.wait_ge(ends_ready, n + 1)
                    pe.matmul(ROWP, pend[:, :], ident[:, :], start=True, stop=True)
                    pe.matmul(ROWH, nz[:, CW - 1:CW], ident[:, :], start=True, stop=True).then_inc(rows_out, 1)
                if u == 4:
                    pe.wait_ge(feat_loaded, 32 * (n + 1))
                    for dx in range(K7):
                        last = pe.matmul(S7, toep[0:MAXROW + H, dx, :], feat[0:MAXROW + H, dx:dx + W],
                                         start=(dx == 0), stop=(dx == K7 - 1))
                    last.then_inc(c7_done, 1)
                    pe.wait_ge(hin_ready, n + 1)
                    pe.matmul(HIN, hin[:, :], ones[0:1, 0:1], start=True, stop=True).then_inc(hin_out, 1)
                if u == 5:
                    pe.wait_ge(hc_ready, n + 1)
                    for r in range(R):
                        last = pe.matmul(Y56, selr[:, r, :], es[:, r * W:(r + 1) * W],
                                         start=(r == 0), stop=(r == R - 1))
                    last.then_inc(y_done, 1)

            def stage_a(n, u):
                if u == 1:
                    group_mean(1, n + 1)
                if u == 2:
                    group_var(1, n + 1)
                if u == 4:
                    pe.wait_ge(fc1_in, n + 1)
                    for h in range(HF):
                        last = pe.matmul(SA[0:RED, 0, 8:10], w1T[:, h, :], fv[:, h, :], start=(h == 0), stop=(h == 1))
                    last.then_inc(fc1_out, 1)
                if u == 5:
                    pe.wait_ge(fc2_in, n + 1)
                    for h in range(HF):
                        last = pe.matmul(SA[:, 0, 10 + h:11 + h], w2T[:, h * P:(h + 1) * P], hs[:, :], start=True, stop=True)
                    last.then_inc(fc2_out, 1)
                if u == GATE0 + GC:
                    pe.wait_ge(red_ready, n + 1)
                    for a in range(2):
                        last = pe.transpose(TR[0:NQ, 0, a * P:(a + 1) * P], red[:, a, :], ident[:, :])
                    last.then_inc(red_turned, 1)

            def work(i, live):
                for u in range(UN):
                    if live.conv:
                        if isinstance(i, int) and i == 0 and u < HF:
                            pe.wait_ge(tern_ready, u + 1)
                        conv(i, u)
                    if isinstance(i, int) and i == 0 and u == 1:
                        pe.wait_ge(w_cnt, 1)
                        pe.matmul(SA[:, 0, 2:4], ones[:, :], wstat[:, 2:4], start=True, stop=True).then_inc(w_cnt_tot, 1)
                        pe.wait_ge(params, 5 * 16)
                        pe.wait_ge(dve_const, 1)
                        pe.wait_ge(toep_ready, 32)
                    if live.b:
                        stage_b(i - 2, u)
                    if live.a:
                        stage_a(i - 1, u)
                    if live.next:
                        if u == 6:
                            if live.a:
                                pe.wait_ge(gate_arg, i)
                            group_mean(0, i + 2)
                        if u == 7:
                            group_var(0, i + 2)
                            if isinstance(i, int) and i == -1:
                                pe.wait_ge(v_ready[0], 1)
                                pe.wait_ge(wa_ready, 1)
                                pe.matmul(SA[:, 0, 0:1], ones[:, :], wstat[:, 0:1], start=True, stop=True).then_inc(w_tot, 1)

            pe.wait_ge(pool_const, 8)
            iterations(pe, NB, work)

            for u in range(STEPS):
                stage_b(LAST - 1, u)
                stage_a(LAST, u)
            for c in range(GC):
                pe.wait_ge(xc_done, GC * LAST + c + 1)
                if c >= 2:
                    pe.wait_ge(row_done, c - 1)
                for h in range(HF):
                    last = pe.matmul(cv[0:1, c % 2, 0:GW], ones[:, 0:1], xc[:, c % 2, h, :], start=(h == 0), stop=(h == 1))
                last.then_inc(row_ready, 1)
            pe.wait_ge(red_ready, NB)
            pe.transpose(TR[0:NQ, 0, P:2 * P], red[:, 1, :], ident[:, :]).then_inc(red_turned, 1)
            for u in range(STEPS):
                stage_b(LAST, u)
            pe.wait_ge(row_loaded, 16)
            pe.wait_ge(row_done, GC)
            for j, c in enumerate(SPREAD):
                if j >= 4:
                    before = SPREAD[j - 4]
                    if before in HELP:
                        pe.wait_ge(g_copied, HELP.index(before) + 1)
                    else:
                        pe.wait_ge(g_used, OWN.index(before) + 1)
                pe.matmul(cv[:, j % 4, 0:CW], ones[0:1, :], row[:, c * CW:(c + 1) * CW],
                          start=True, stop=True).then_inc(g_rows, 1)
            pe.wait_ge(w_done, CH * NB)

            def phase2(q, s):
                t, k = RING * q + s, s % ROWS
                pe.wait_ge(grow_loaded[k], 16 * (RING // ROWS * q + s // ROWS + 1))
                for c2 in range(CH // 2):
                    wait(pe, prod_done, N2 * t + HF * (c2 - 1))
                    for e in range(2):
                        last = pe.matmul(cv[:, 2 * (c2 % 2) + e, 0:CW], ones[32 * k:32 * k + 1, :],
                                         growt[32 * k:32 * k + 1, (2 * c2 + e) * CW:(2 * c2 + e + 1) * CW],
                                         start=True, stop=True)
                    last.then_inc(spread, 1)

            steps(pe, NB, phase2)

        @block.vector
        def _(v):
            v.memset(rmask[:, :], 1.0)
            v.drain()
            v.memset(rmask[:, 0:P:CH], 0.0)
            v.wait_ge(pool_const, 8)
            v.tensor_scalar(pj[:, :], pidx[:, :], CH - 1, None, ALU.bitwise_and)
            v.drain()
            v.tensor_copy(pjf[:, :], pj[:, :])
            v.drain()
            for r in range(R):
                v.tensor_scalar(tgt[:, r:r + 1], pjf[:, :], float(R), float(r), ALU.mult, ALU.add)
            v.drain()
            for r in range(R):
                last = v.tensor_scalar(selr[:, r, :], iot[:, :], tgt[:, r:r + 1], None, ALU.is_equal)
            last.then_inc(dve_const, 1)

            def threshold():
                v.wait_ge(w_loaded, 16)
                v.wait_ge(w_tot, 1)
                v.tensor_scalar(wstat[:, 1:2], SA[:, 0, 0:1], 1.0 / (WCOLS * P), 0.7, ALU.mult, ALU.mult)
                v.drain()
                v.tensor_scalar(wstat[:, 4:5], wstat[:, 1:2], -1.0, None, ALU.mult)
                v.drain()
                v.tensor_scalar(wj, wv, wstat[:, 4:5], None, ALU.is_le)

            def ternary(o):
                part = lambda a: a.rearrange("p (t k m) -> p t k m", t=TAPS, k=HF)[:, :, :, o * P:(o + 1) * P]
                v.scalar_tensor_tensor(tern[:, :, :, o * P:(o + 1) * P], part(wv), wstat[:, 1:2], part(wj),
                                       ALU.is_ge, ALU.subtract).then_inc(tern_ready, 1)

            def bands():
                v.wait_ge(lw_loaded, 16)
                v.wait_ge(pool_zero, 4)
                for c in range(2):
                    a = c * MAXROW
                    for dy in range(K7):
                        last = v.tensor_copy(band[a:a + H, :, H - 1 + PAD7 - dy], lw[a:a + H, dy, :, c])
                last.then_inc(band_ready, 1)

            def count_kept():
                v.wait_ge(wa_ready, 1)
                v.drain()
                v.tensor_scalar(wj, wa, wstat[:, 1:2], None, ALU.is_gt, ALU.add, accum_out=wstat[:, 3:4])
                v.drain()
                v.scalar_tensor_tensor(wj, wa, wstat[:, 1:2], wa, ALU.is_gt, ALU.mult,
                                       accum_out=wstat[:, 2:3]).then_inc(w_cnt, 1)

            def scale_of_weights():
                v.wait_ge(w_cnt_tot, 1)
                v.tensor_copy(wstat[:, 5:7], SA[:, 0, 2:4])
                v.drain()
                v.reciprocal(wstat[:, 7:8], wstat[:, 6:7])
                v.drain()
                v.tensor_tensor(alpha[:, :], wstat[:, 5:6], wstat[:, 7:8], ALU.mult).then_inc(w_ready, 1)
                v.wait_ge(params, 5 * 16)

            def held(sem_, value):
                v.drain()
                v.wait_ge(sem_, value)
                v.memset(tick[:, :], 0.0)

            def x_stats(n, cs):
                held(x_loaded, 16 * (n + 1))
                for c in cs:
                    for h in range(HF):
                        v.bn_stats(st[0][:, h, c, :], chunk(n % SLOTS, h, c))

            def x1_stats(n, b):
                held(x1_done, UN * n + 2 * b + 2)
                for h in range(HF):
                    v.bn_stats(st[1][:, h, b, :], chunk(n % SLOTS, h, b))
                v.tensor_reduce(mx1[:, b, :], xs[:, n % SLOTS, :, b * CW:(b + 1) * CW], AX_X, ALU.max)

            def gn_aggregate(q):
                v.drain()
                for h in range(HF):
                    last = v.bn_aggr(mv[q][:, h, :], st[q][:, h, :, :].rearrange("p c s -> p (c s)"))
                last.then_inc(mean_in[q], 1)

            def gn_deviation(q, count):
                v.wait_ge(mean_out[q], count)
                v.tensor_copy(gm[q][:, :], SA[:, 0, 4 * q:4 * q + 2])
                v.drain()
                v.tensor_tensor(dq[q][:, :], mv[q][:, :, 0], gm[q][:, :], ALU.subtract)
                v.drain()
                v.tensor_tensor(dq[q][:, :], dq[q][:, :], dq[q][:, :], ALU.mult)
                v.drain()
                v.tensor_tensor(dv[q][:, :], dq[q][:, :], mv[q][:, :, 1], ALU.add).then_inc(var_in[q], 1)

            def gn_variance(q, count):
                v.wait_ge(var_out[q], count)
                v.tensor_scalar(vv[q][:, :], SA[:, 0, 4 * q + 2:4 * q + 4], 1e-5, None, ALU.add).then_inc(v_ready[q], 1)

            def newton(q, count):
                v.wait_ge(rs_guess[q], count)
                v.tensor_tensor(nt[q][:, :], r0[q][:, :], r0[q][:, :], ALU.mult)
                v.drain()
                v.tensor_tensor(nt[q][:, :], nt[q][:, :], vv[q][:, :], ALU.mult)
                v.drain()
                v.tensor_scalar(nt[q][:, :], nt[q][:, :], -0.5, 1.5, ALU.mult, ALU.add)
                v.drain()
                v.tensor_tensor(rs[q][:, :], r0[q][:, :], nt[q][:, :], ALU.mult)
                v.drain()

            def channels(n, c):
                v.wait_ge(xc_done, GC * n + c + 1)
                v.tensor_tensor(xp[:, 1, :], xc[:, c % 2, 0, :], xc[:, c % 2, 1, :], ALU.max).then_inc(pair_max_done, 1)
                v.drain()
                v.wait_ge(pair_sum_done, GC * n + c + 1)
                for a in range(2):
                    last = v.transpose(xt[:, a, :], xp[:, a, :])
                last.then_inc(turned, 1)
                v.drain()
                for a, op in enumerate((ALU.add, ALU.max)):
                    last = v.tensor_reduce(red[:, a, c * GB:(c + 1) * GB], xt[:, a, :].rearrange("p (b x) -> p b x", x=SQ),
                                           AX_X, op)
                if c == GC - 1:
                    last.then_inc(red_ready, 1)

            def channel_maps(n):
                v.wait_ge(red_turned, n + 1)
                if not isinstance(n, int) or n > 0:
                    v.wait_ge(maps_stored, 16 * n)
                v.tensor_reduce(maps[:, 0, :], TRv[:, 0, :, :], AX_X, ALU.add)
                v.tensor_reduce(maps[:, 1, :], TRv[:, 1, :, :], AX_X, ALU.max)
                v.drain()
                v.tensor_scalar(maps[:, 0, :], maps[:, 0, :], 1.0 / (HF * P), None, ALU.mult).then_inc(maps_ready, 1)

            def bn_count(c, buf):
                for h in range(HF):
                    last = v.bn_stats(stw[:, h, c, :], buf[:, h, :])
                last.then_inc(w_done, 1)

            def bn_product(n, c, g, buf):
                for h in range(HF):
                    last = v.scalar_tensor_tensor(buf[:, h, :], chunk(n % SLOTS, h, c), gmA[:, n, h:h + 1], g,
                                                  ALU.subtract, ALU.mult)
                return last

            def bn_aggregate(n):
                v.drain()
                for h in range(HF):
                    v.bn_aggr(mwt[:, h, :], stw[:, h, :, :].rearrange("p c s -> p (c s)"))
                v.drain()
                v.tensor_copy(mwA[:, n, :, :], mwt[:, :, :])

            def bn_chunk(n, c):
                if c == 0:
                    v.wait_ge(g_spread, 16 * (n + 1))
                bn_product(n, c, gB[:, c * CW:(c + 1) * CW], wk[:, c % 2])
                v.drain()
                bn_count(c, wk[:, c % 2])
                if c == CH - 1:
                    bn_aggregate(n)

            def stage_b(n, u):
                if u == 0:
                    v.wait_ge(ms_loaded, 16 * (n + 1))
                    v.tensor_scalar(zs[:, :], ms[:, :], sv[:, 5:6], sv[:, 6:7], ALU.mult, ALU.add).then_inc(ms_read, 1)
                    v.drain()
                    v.scalar_tensor_tensor(nz[:, :], zs[:, :], -1.0, zs[:, :], ALU.mult, ALU.min).then_inc(nz_ready, 1)
                if u == 1:
                    v.wait_ge(e_ready, n + 1)
                    v.tensor_scalar(us[:, :], es[:, :], 1.0, None, ALU.add).then_inc(u_ready, 1)
                    v.drain()
                    v.scalar_tensor_tensor(de[:, :], us[:, :], 1.0, es[:, :], ALU.subtract, ALU.subtract)
                    v.drain()
                    v.scalar_tensor_tensor(zs[:, :], zs[:, :], 0.0, de[:, :], ALU.max, ALU.subtract)
                    v.drain()
                if u == 2:
                    v.wait_ge(l_ready, n + 1)
                    v.scalar_tensor_tensor(de[:, :], zs[:, :], 1.0, ls[:, :], ALU.mult, ALU.add,
                                           accum_out=sumd[:, :]).then_inc(delta_ready, 1)
                    v.tensor_scalar(us[:, :], ms[:, :], sv[:, 1:2], sv[:, 2:3], ALU.mult, ALU.add)
                    v.drain()
                    v.tensor_tensor(zs[:, :], de[:, :], ms[:, :], ALU.mult)
                    v.drain()
                    v.tensor_tensor(ls[:, :], zs[:, :], us[:, :], ALU.mult)
                    v.drain()
                if u == 3:
                    v.wait_ge(decay_ready, n + 1)
                    v.tensor_tensor_scan(nz[:, :], dA[:, :], ls[:, :], 0.0, ALU.mult, ALU.add).then_inc(ends_ready, 1)
                if u == 4:
                    v.wait_ge(rows_out, n + 1)
                    v.tensor_tensor(rp[:, :], ROWP, rmask[:, :], ALU.mult)
                    v.tensor_copy(rh[:, :], ROWH)
                    v.drain()
                    v.tensor_tensor_scan(rH[:, :], rp[:, :], rh[:, :], 0.0, ALU.mult, ALU.add)
                    v.drain()
                    v.tensor_tensor(hin[:, 1:P], rH[:, 0:P - 1], rmask[:, 1:P], ALU.mult).then_inc(hin_ready, 1)
                if u == 5:
                    v.wait_ge(c7_done, n + 1)
                    v.tensor_scalar(sy[:, 1, :], S7, CLAMP, None, ALU.max).then_inc(s_taken, 1)
                    v.tensor_scalar(us[:, :], ms[:, :], sv[:, 3:4], sv[:, 4:5], ALU.mult, ALU.add)
                    v.wait_ge(hin_out, n + 1)
                    v.tensor_copy(hinc[:, :], HIN)
                    v.drain()
                    v.tensor_tensor_scan(zs[:, :], dA[:, :], ls[:, :], hinc[:, 0:1], ALU.mult, ALU.add)
                    v.drain()
                    v.tensor_tensor(es[:, :], zs[:, :], us[:, :], ALU.mult).then_inc(hc_ready, 1)
                if u == 6:
                    v.wait_ge(y_done, n + 1)
                    v.tensor_scalar(sy[:, 0, :], Y56, CLAMP, None, ALU.max).then_inc(sy_ready, 1)
                if u == 7:
                    v.wait_ge(sye_ready, n + 1)
                    v.tensor_scalar(syd[:, :, :], sye[:, :, :], 1.0, None, ALU.add)
                    v.drain()
                    v.reciprocal(syr[:, :, :], syd[:, :, :])
                    v.drain()
                    v.tensor_tensor(g56[:, :], syr[:, 0, :], syr[:, 1, :], ALU.add).then_inc(g_ready, 1)
            def stage_a(n, u):
                if u == 0:
                    x1_stats(n, CH - 1)
                if u == 1:
                    gn_aggregate(1)
                if u == 2:
                    v.tensor_reduce(fmx[:, :], mx1[:, :, :].rearrange("p c h -> p h c"), AX_X, ALU.max)
                    gn_deviation(1, n + 1)
                if u == 3:
                    gn_variance(1, n + 1)
                    v.tensor_copy(gmA[:, n, :], gm[1][:, :])
                    v.tensor_tensor(fd[:, :, 0], mv[1][:, :, 0], gm[1][:, :], ALU.subtract)
                    v.tensor_tensor(fd[:, :, 1], fmx[:, :], gm[1][:, :], ALU.subtract)
                    v.drain()
                if u == 4:
                    newton(1, n + 1)
                    for h in range(HF):
                        last = v.tensor_scalar(fv[:, h, :], fd[:, h, :], rs[1][:, h:h + 1], None, ALU.mult)
                    last.then_inc(fc1_in, 1)
                if u == 5:
                    v.wait_ge(fc1_out, n + 1)
                    v.tensor_scalar(hr[:, :], SA[0:RED, 0, 8:10], 0.0, None, ALU.max)
                    v.drain()
                    v.tensor_tensor(hs[:, :], hr[:, 0:1], hr[:, 1:2], ALU.add).then_inc(fc2_in, 1)
                if u == 6:
                    v.wait_ge(fc2_out, n + 1)
                    v.tensor_scalar(garg[:, :], SA[:, 0, 10:12], CLAMP, None, ALU.max).then_inc(gate_arg, 1)
                if u == 7:
                    v.wait_ge(gate_exp, n + 1)
                    v.tensor_scalar(gden[:, :], gexp[:, :], 1.0, None, ALU.add)
                    v.drain()
                    v.reciprocal(gate[:, :], gden[:, :])
                    v.drain()
                    v.tensor_tensor(kcur[:, :], gate[:, :], rs[1][:, :], ALU.mult)
                    v.drain()
                    v.scalar_tensor_tensor(nb[:, :], gm[1][:, :], -1.0, kcur[:, :], ALU.mult, ALU.mult).then_inc(gate_done, 1)
                    v.tensor_copy(kA[:, n, :], kcur[:, :])
                if u == GATE0 + GC + 1:
                    channel_maps(n)

            def stage_next_small(n, u):
                if u == 5:
                    gn_aggregate(0)
                if u == 7:
                    gn_deviation(0, n + 1)
                if u == 8:
                    gn_variance(0, n + 1)
                    if isinstance(n, int) and n == 0:
                        threshold()
                if u == 9:
                    newton(0, n + 1)
                    v.scalar_tensor_tensor(nbx[:, :], gm[0][:, :], -1.0, rs[0][:, :], ALU.mult, ALU.mult).then_inc(norm_ready, 1)

            def stage_next(n, u):
                if u == 3:
                    x_stats(n, range(CH // 2))
                if u == 4:
                    x_stats(n, range(CH // 2, CH))
                if isinstance(n, int) and n == 0 and u == 9:
                    ternary(0)
                    ternary(1)
                    bands()
                    count_kept()

            def work(i, live):
                for u in range(UN):
                    if isinstance(i, int) and i == 0 and u == 0:
                        scale_of_weights()
                    if live.next:
                        stage_next_small(i + 1, u)
                    if live.b:
                        stage_b(i - 2, u)
                    if live.a:
                        stage_a(i - 1, u)
                    if live.next:
                        stage_next(i + 1, u)
                    if live.b:
                        for c in WSTAT.get(u, []):
                            bn_chunk(i - 2, c)
                    if live.conv and u > 0 and u % 2 == 0:
                        x1_stats(i, u // 2 - 1)
                    if live.a and GATE0 <= u < GATE0 + GC:
                        channels(i - 1, u - GATE0)

            iterations(v, NB, work)

            for u in range(STEPS):
                stage_b(LAST - 1, u)
                stage_a(LAST, u)
            for c in range(GC):
                v.wait_ge(xc_done, GC * LAST + c + 1)
                v.tensor_tensor(xp[:, 1, :], xc[:, c % 2, 0, :], xc[:, c % 2, 1, :], ALU.max).then_inc(pair_max_done, 1)
                v.drain()
                v.transpose(xt[:, 1, :], xp[:, 1, :])
                v.drain()
                last = v.tensor_reduce(red[:, 1, c * GB:(c + 1) * GB], xt[:, 1, :].rearrange("p (b x) -> p b x", x=SQ),
                                       AX_X, ALU.max)
            last.then_inc(red_ready, 1)
            for k in range(2):
                last = v.tensor_scalar(ngm[:, k, :], gmA[:, LAST - k, :], -1.0, None, ALU.mult)
            last.then_inc(ngm_ready, 1)
            v.wait_ge(red_turned, NB)
            v.wait_ge(maps_stored, 16 * LAST)
            v.tensor_reduce(maps[:, 1, :], TRv[:, 1, :, :], AX_X, ALU.max).then_inc(maps_ready, 1)

            def bn_made(c):
                v.wait_ge(w_made, c + 1)
                bn_count(c, w_ring[c % len(w_ring)])

            for c in BEFORE_B:
                bn_made(c)
            for u in range(STEPS):
                stage_b(LAST, u)
                for c in WITHIN_B.get(u, []):
                    bn_made(c)
                    if c == CH - 1:
                        bn_aggregate(LAST - 1)
            for k, c in enumerate(OWN):
                j = SPREAD.index(c)
                v.wait_ge(g_rows, j + 1)
                bn_product(LAST, c, cv[:, j % 4, 0:CW], wk[:, k % 2]).then_inc(g_used, 1)
                v.drain()
                bn_count(c, wk[:, k % 2])
            for k, c in enumerate(HELP):
                v.wait_ge(w_made, CH + k + 1)
                bn_count(c, w_help[k])
            bn_aggregate(LAST)

            v.drain()
            v.tensor_tensor(bm[:, :, :], mwA[:, :, :, 0], kA[:, :, :], ALU.mult)
            v.tensor_tensor(bq[:, :, :], mwA[:, :, :, 1], kA[:, :, :], ALU.mult)
            v.drain()
            v.tensor_tensor(bq[:, :, :], bq[:, :, :], kA[:, :, :], ALU.mult)
            v.tensor_reduce(bs[:, :], bm[:, :, :].rearrange("p n h -> p h n"), AX_X, ALU.add)
            v.drain()
            v.tensor_scalar(bmean[:, :], bs[:, :], 1.0 / NB, None, ALU.mult)
            v.drain()
            for h in range(HF):
                v.tensor_scalar(bm[:, :, h], bm[:, :, h], bmean[:, h:h + 1], None, ALU.subtract)
            v.drain()
            v.tensor_tensor(bm[:, :, :], bm[:, :, :], bm[:, :, :], ALU.mult)
            v.drain()
            v.tensor_tensor(bq[:, :, :], bq[:, :, :], bm[:, :, :], ALU.add)
            v.drain()
            v.tensor_reduce(bs[:, :], bq[:, :, :].rearrange("p n h -> p h n"), AX_X, ALU.add)
            v.drain()
            v.tensor_scalar(vv[2][:, :], bs[:, :], 1.0 / NB, 1e-5, ALU.mult, ALU.add).then_inc(v_ready[2], 1)
            newton(2, 1)
            v.tensor_tensor(bscale[:, :], rs[2][:, :], bnp[:, 0, :], ALU.mult)
            v.drain()
            for h in range(HF):
                v.tensor_scalar(bA[:, :, h], kA[:, :, h], bscale[:, h:h + 1], None, ALU.mult)
            v.tensor_tensor(bs[:, :], bmean[:, :], bscale[:, :], ALU.mult)
            v.drain()
            v.tensor_tensor(bB[:, :], bnp[:, 1, :], bs[:, :], ALU.subtract).then_inc(bn_ready, 1)

            def product(t, s, c2, h, n):
                if h == 0:
                    v.wait_ge(spread, (CH // 2) * t + c2 + 1)
                wait(v, *(added(t, c2 - 2, h) if c2 >= 2 else added(t - 1, c2 - 2 + CH // 2, h)))
                buf = step_buf((N2 * s + HF * c2 + h) % RING2)
                pair_ = cv[:, 2 * (c2 % 2):2 * (c2 % 2) + 2, 0:CW]
                v.wait_ge(bn_ready, 1)
                v.scalar_tensor_tensor(buf.rearrange("p (e c) -> p e c", e=2),
                                       pixels(s, h, c2).rearrange("p (e c) -> p e c", e=2),
                                       gmA[:, n, h:h + 1], pair_, ALU.subtract, ALU.mult).then_inc(prod_done, 1)

            def add(t, s, c2):
                k = N2 * t + HF * c2
                v.wait_ge(act_done, k + 1)
                at = pixels(s, 0, c2)
                v.tensor_tensor(at, at, step_buf((N2 * s + HF * c2) % RING2), ALU.add).then_inc(add_dve, 1)

            def phase2(q, s):
                t, n = RING * q + s, image_of(q, s)
                wait(v, x1_back[s], 16 * PIECES[s] * (q if s < SLOTS else q + 1) + (16 if s == SLOTS else 0))
                v.tensor_copy(bAs[:, s, :], bA[:, n, :])
                for c2 in range(CH // 2):
                    product(t, s, c2, 0, n)
                    product(t, s, c2, 1, n)
                    if c2 > 0 and not by_pool(c2 - 1, 0):
                        add(t, s, c2 - 1)
                add(t, s, CH // 2 - 1)

            steps(v, NB, phase2)


def kernel(**inputs):
    import numpy as np
    import concourse.bacc as bacc
    from concourse.bass_utils import run_bass_kernel_spmd

    x = np.asarray(inputs["x"])
    n = x.shape[0]
    halves = lambda a: np.ascontiguousarray(np.asarray(a).reshape(2, P).T)
    by_state = lambda a: np.repeat(np.asarray(a).reshape(-1), CH)
    every = lambda a: np.repeat(np.asarray(a).reshape(-1), P)
    w1 = np.asarray(inputs["L1_conv_ca_w1"])
    arrays = {
        "x": np.ascontiguousarray(x.reshape(n, PX, 2, P).transpose(0, 2, 3, 1)),
        "w": np.ascontiguousarray(np.asarray(inputs["L0_conv_W"]).reshape(TAPS * 2, P, 2 * P)),
        "bias": halves(inputs["L0_conv_b"]),
        "w1": np.ascontiguousarray(w1.T.reshape(2, P, RED).transpose(1, 0, 2)),
        "w2": np.ascontiguousarray(np.asarray(inputs["L1_conv_ca_w2"]).T),
        "lsa": np.ascontiguousarray(np.asarray(inputs["L1_conv_lsa_w"]).reshape(-1)),
        "scal": np.ascontiguousarray(np.stack(
            [by_state(inputs["L1_conv_A"]), by_state(inputs["L1_conv_B_w"]), by_state(inputs["L1_conv_B_b"]),
             by_state(inputs["L1_conv_C_w"]), by_state(inputs["L1_conv_C_b"]),
             every(inputs["L1_conv_d_w"]), every(inputs["L1_conv_d_b"])], axis=1)),
        "bn": np.ascontiguousarray(np.stack([halves(inputs["L1_conv_bn_gamma"]), halves(inputs["L1_conv_bn_beta"])], axis=1)),
    }
    nc = bacc.Bacc("TRN2", target_bir_lowering=False, num_devices=1)
    args = [nc.dram_tensor(f"in_{k}", a.shape, F32, kind="ExternalInput").ap() for k, a in arrays.items()]
    out = nc.dram_tensor("out", (n, 2, P, PX), F32, kind="ExternalOutput").ap()
    by_name = dict(zip(arrays, args))
    build_kernel(nc, by_name["x"], by_name["w"], by_name["bias"], by_name["w1"], by_name["w2"], by_name["lsa"],
                 by_name["scal"], by_name["bn"], out)
    r = run_bass_kernel_spmd(nc, [{f"in_{k}": a for k, a in arrays.items()}], core_ids=[0])
    got = r.results[0]["out"]
    return np.ascontiguousarray(got.reshape(n, 2, P, PX).transpose(0, 3, 1, 2).reshape(n, H, W, 2 * P))
```
